# Optimizing a Trainium2 kernel written in Bass

```python
import numpy as np
import jax
import jax.numpy as jnp

def _softmax(x, axis=-1):
    return jax.nn.softmax(x, axis=axis)
def _gelu(x):
    return jax.nn.gelu(x, approximate=True)
def _silu(x):
    return jax.nn.silu(x)
def _sigmoid(x):
    return jax.nn.sigmoid(x)
def _layernorm(x, axis=-1, eps=1e-5):
    m = jnp.mean(x, axis=axis, keepdims=True)
    v = jnp.var(x, axis=axis, keepdims=True)
    return (x - m) / jnp.sqrt(v + eps)
def _scatter_add(tgt, idx, src, axis=0):
    return tgt.at[idx].add(src)
def _segment_sum(src, seg, n):
    return jax.ops.segment_sum(src, seg, n)

kernel_name = 'mk_conv_seq_d2_conv_nchw512_39b11b'

def setup_inputs(seed: int = 0):
    np.random.seed(seed)
    _w = jnp.asarray
    def _rec_inputs():
        import jax
        import jax.numpy as jnp
        _gk = jax.random.key(seed)
        x = -0.0002928 + 1 * jax.random.normal(jax.random.fold_in(_gk, 1), (8, 512, 32, 32), jnp.float32)
        return x
    x = _rec_inputs()
    def _L0_conv_setup():
        import math
        import jax, jax.numpy as jnp
        import numpy as np
        NUM_HEADS = 8
        GROUPS = 32
        EPS = 1e-05

        def group_norm(x, w, b):
            B, C, H, W = x.shape
            xg = x.reshape(B, GROUPS, C // GROUPS, H, W)
            mu = xg.mean(axis=(2, 3, 4), keepdims=True)
            var = xg.var(axis=(2, 3, 4), keepdims=True)
            xn = ((xg - mu) * jax.lax.rsqrt(var + EPS)).reshape(B, C, H, W)
            return xn * w[None, :, None, None] + b[None, :, None, None]
        key = jax.random.key(seed)
        ks = jax.random.split(key, 3)
        B, C, H, W = (8, 512, 32, 32)
        x = jax.random.normal(ks[0], (B, C, H, W), dtype=jnp.float32)
        norm_w = jnp.ones((C,), jnp.float32)
        norm_b = jnp.zeros((C,), jnp.float32)
        qkv_w = jax.random.normal(ks[1], (3 * C, C), dtype=jnp.float32) * (1.0 / math.sqrt(C))
        qkv_b = jnp.zeros((3 * C,), jnp.float32)
        proj_w = jax.random.normal(ks[2], (C, C), dtype=jnp.float32) * (1.0 / math.sqrt(C))
        proj_b = jnp.zeros((C,), jnp.float32)
        return {'x': x, 'norm_w': norm_w, 'norm_b': norm_b, 'qkv_w': qkv_w, 'qkv_b': qkv_b, 'proj_w': proj_w, 'proj_b': proj_b}
    _L0_conv_all = _L0_conv_setup()
    _L0_conv_in = {k: v for k, v in _L0_conv_all.items() if k in ('norm_w', 'norm_b', 'qkv_w', 'qkv_b', 'proj_w', 'proj_b', )}
    del _L0_conv_all

    def _L1_conv_setup():
        import jax, jax.numpy as jnp
        import numpy as np
        NUM_GROUPS = 32
        EPS = 1e-06

        def group_norm(x, gamma, beta):
            b, c, h, w = x.shape
            xg = x.reshape(b, NUM_GROUPS, c // NUM_GROUPS, h, w)
            mean = xg.mean(axis=(2, 3, 4), keepdims=True)
            var = xg.var(axis=(2, 3, 4), keepdims=True)
            xg = (xg - mean) * jax.lax.rsqrt(var + EPS)
            x = xg.reshape(b, c, h, w)
            return x * gamma[None, :, None, None] + beta[None, :, None, None]

        def conv1x1(x, w, bias):
            return jnp.einsum('bchw,oc->bohw', x, w) + bias[None, :, None, None]
        key = jax.random.key(seed)
        ks = jax.random.split(key, 6)
        B, C, H, W = (1, 512, 96, 96)
        std = 1.0 / np.sqrt(C)
        return {'x': jax.random.normal(ks[0], (B, C, H, W), dtype=jnp.float32), 'gn_gamma': jnp.ones((C,), dtype=jnp.float32), 'gn_beta': jnp.zeros((C,), dtype=jnp.float32), 'q_w': jax.random.normal(ks[1], (C, C), dtype=jnp.float32) * std, 'q_b': jnp.zeros((C,), dtype=jnp.float32), 'k_w': jax.random.normal(ks[2], (C, C), dtype=jnp.float32) * std, 'k_b': jnp.zeros((C,), dtype=jnp.float32), 'v_w': jax.random.normal(ks[3], (C, C), dtype=jnp.float32) * std, 'v_b': jnp.zeros((C,), dtype=jnp.float32), 'proj_w': jax.random.normal(ks[4], (C, C), dtype=jnp.float32) * std, 'proj_b': jnp.zeros((C,), dtype=jnp.float32)}
    _L1_conv_all = _L1_conv_setup()
    _L1_conv_in = {k: v for k, v in _L1_conv_all.items() if k in ('gn_gamma', 'gn_beta', 'q_w', 'q_b', 'k_w', 'k_b', 'v_w', 'v_b', 'proj_w', 'proj_b', )}
    del _L1_conv_all

    return {
        "x": x,
        "L0_conv_norm_w": _L0_conv_in["norm_w"],
        "L0_conv_norm_b": _L0_conv_in["norm_b"],
        "L0_conv_qkv_w": _L0_conv_in["qkv_w"],
        "L0_conv_qkv_b": _L0_conv_in["qkv_b"],
        "L0_conv_proj_w": _L0_conv_in["proj_w"],
        "L0_conv_proj_b": _L0_conv_in["proj_b"],
        "L1_conv_gn_gamma": _L1_conv_in["gn_gamma"],
        "L1_conv_gn_beta": _L1_conv_in["gn_beta"],
        "L1_conv_q_w": _L1_conv_in["q_w"],
        "L1_conv_q_b": _L1_conv_in["q_b"],
        "L1_conv_k_w": _L1_conv_in["k_w"],
        "L1_conv_k_b": _L1_conv_in["k_b"],
        "L1_conv_v_w": _L1_conv_in["v_w"],
        "L1_conv_v_b": _L1_conv_in["v_b"],
        "L1_conv_proj_w": _L1_conv_in["proj_w"],
        "L1_conv_proj_b": _L1_conv_in["proj_b"],
    }

def reference(x, L0_conv_norm_w, L0_conv_norm_b, L0_conv_qkv_w, L0_conv_qkv_b, L0_conv_proj_w, L0_conv_proj_b, L1_conv_gn_gamma, L1_conv_gn_beta, L1_conv_q_w, L1_conv_q_b, L1_conv_k_w, L1_conv_k_b, L1_conv_v_w, L1_conv_v_b, L1_conv_proj_w, L1_conv_proj_b):
    import jax
    import jax.numpy as jnp
    def _L0_conv_ref(x, norm_w, norm_b, qkv_w, qkv_b, proj_w, proj_b):
        import math
        import jax, jax.numpy as jnp
        import numpy as np
        NUM_HEADS = 8
        GROUPS = 32
        EPS = 1e-05

        def group_norm(x, w, b):
            B, C, H, W = x.shape
            xg = x.reshape(B, GROUPS, C // GROUPS, H, W)
            mu = xg.mean(axis=(2, 3, 4), keepdims=True)
            var = xg.var(axis=(2, 3, 4), keepdims=True)
            xn = ((xg - mu) * jax.lax.rsqrt(var + EPS)).reshape(B, C, H, W)
            return xn * w[None, :, None, None] + b[None, :, None, None]
        B, C, H, W = x.shape
        T = H * W
        heads = NUM_HEADS
        ch = C // heads
        xn = group_norm(x, norm_w, norm_b)
        qkv = jnp.einsum('oc,bchw->bohw', qkv_w, xn).reshape(B, 3 * C, T) + qkv_b[None, :, None]
        qkv = qkv.reshape(B * heads, 3 * ch, T)
        q, k, v = jnp.split(qkv, 3, axis=1)
        scale = 1.0 / math.sqrt(math.sqrt(ch))
        w = jnp.einsum('bct,bcs->bts', q * scale, k * scale)
        w = jax.nn.softmax(w.astype(jnp.float32), axis=-1).astype(qkv.dtype)
        a = jnp.einsum('bts,bcs->bct', w, v)
        h = a.reshape(B, C, H, W)
        h = jnp.einsum('oc,bchw->bohw', proj_w, h) + proj_b[None, :, None, None]
        return x + h

    def _L1_conv_ref(x, gn_gamma, gn_beta, q_w, q_b, k_w, k_b, v_w, v_b, proj_w, proj_b):
        import jax, jax.numpy as jnp
        import numpy as np
        NUM_GROUPS = 32
        EPS = 1e-06

        def group_norm(x, gamma, beta):
            b, c, h, w = x.shape
            xg = x.reshape(b, NUM_GROUPS, c // NUM_GROUPS, h, w)
            mean = xg.mean(axis=(2, 3, 4), keepdims=True)
            var = xg.var(axis=(2, 3, 4), keepdims=True)
            xg = (xg - mean) * jax.lax.rsqrt(var + EPS)
            x = xg.reshape(b, c, h, w)
            return x * gamma[None, :, None, None] + beta[None, :, None, None]

        def conv1x1(x, w, bias):
            return jnp.einsum('bchw,oc->bohw', x, w) + bias[None, :, None, None]
        b, c, h, w = x.shape
        hn = group_norm(x, gn_gamma, gn_beta)
        q = conv1x1(hn, q_w, q_b).reshape(b, c, h * w)
        k = conv1x1(hn, k_w, k_b).reshape(b, c, h * w)
        v = conv1x1(hn, v_w, v_b).reshape(b, c, h * w)
        scale = jnp.asarray(c, x.dtype) ** (-0.5)
        scores = jnp.einsum('bci,bcj->bij', q, k) * scale
        attn = jax.nn.softmax(scores, axis=-1)
        out = jnp.einsum('bcj,bij->bci', v, attn).reshape(b, c, h, w)
        out = conv1x1(out, proj_w, proj_b)
        return x + out

    def _gn(v, G=32, eps=1e-5):
        B_, C_, H_, W_ = v.shape
        g = v.reshape(B_, G, C_ // G, H_, W_)
        m = jnp.mean(g, axis=(2, 3, 4), keepdims=True)
        s = jnp.var(g, axis=(2, 3, 4), keepdims=True)
        return ((g - m) / jnp.sqrt(s + eps)).reshape(v.shape)

    def _ln_c(v, eps=1e-6):
        m = jnp.mean(v, axis=1, keepdims=True)
        s = jnp.var(v, axis=1, keepdims=True)
        return (v - m) / jnp.sqrt(s + eps)

    def _ln_t(v, eps=1e-5):
        m = jnp.mean(v, axis=-1, keepdims=True)
        s = jnp.var(v, axis=-1, keepdims=True)
        return (v - m) / jnp.sqrt(s + eps)

    def _to_tokens(v):
        B_, C_, H_, W_ = v.shape
        return v.reshape(B_, C_, H_ * W_).transpose(0, 2, 1)
    def _from_tokens(t, like):
        B_, C_, H_, W_ = like.shape
        return t.transpose(0, 2, 1).reshape(B_, C_, H_, W_)

    x = _L0_conv_ref(x, L0_conv_norm_w, L0_conv_norm_b, L0_conv_qkv_w, L0_conv_qkv_b, L0_conv_proj_w, L0_conv_proj_b)
    x = _L1_conv_ref(x, L1_conv_gn_gamma, L1_conv_gn_beta, L1_conv_q_w, L1_conv_q_b, L1_conv_k_w, L1_conv_k_b, L1_conv_v_w, L1_conv_v_b, L1_conv_proj_w, L1_conv_proj_b)
    return x


_drawn_inputs = setup_inputs


def setup_inputs(seed=0):
    import zlib

    import numpy as np

    out = dict(_drawn_inputs(seed))
    spreads = {'L0_conv_norm_w': (1.0, 0.2),
     'L0_conv_norm_b': (0.0, 0.1),
     'L0_conv_qkv_b': (0.0, 0.1),
     'L0_conv_proj_b': (0.0, 0.1),
     'L1_conv_gn_gamma': (1.0, 0.2),
     'L1_conv_gn_beta': (0.0, 0.1),
     'L1_conv_q_b': (0.0, 0.8),
     'L1_conv_k_b': (0.0, 0.8),
     'L1_conv_v_b': (0.0, 0.1),
     'L1_conv_proj_b': (0.0, 0.1)}
    factors = {}
    for name, (base, spread) in spreads.items():
        noise = np.random.default_rng([zlib.crc32(name.encode()), seed]).standard_normal(out[name].shape)
        drawn = base * np.exp(spread * noise) if base else spread * noise
        out[name] = jnp.asarray(drawn.astype(out[name].dtype))
    for name, factor in factors.items():
        out[name] = (out[name] * factor).astype(out[name].dtype)
    return out
```

```python
from contextlib import ExitStack

import numpy as np
import concourse.bass as bass
from concourse import mybir

F32 = mybir.dt.float32
F16 = mybir.dt.float16
ALU = mybir.AluOpType
ACT = mybir.ActivationFunctionType
AX = mybir.AxisListType
ABSMAX = bass.bass_isa.ReduceOp.max

P = 128
B, C, T = 8, 512, 1024
CT = C // P
TT = T // P
HALF = 512
HEADS = 8
CH = C // HEADS
PAIRS = HEADS // 2
GROUP = C // 32
EPS0, EPS1 = 1e-5, 1e-6

WSC = 512.0
ZSC = 64.0
QSC = 1.0 / (WSC * ZSC * 2)
PSC = 4096.0

UNITS_PAIR = 2 * TT
UNITS0 = PAIRS * UNITS_PAIR
UNITS = UNITS0 + TT
QUARTERS = TT // 2
PV_PAIR = QUARTERS
PV0 = PAIRS * PV_PAIR
PVS = PV0 + 2 * QUARTERS
FILL = 6
G_PROJ0 = (PAIRS - 1) * FILL
G_PROJ1 = G_PROJ0 + CT
G_G = G_PROJ1 + CT
G_U = G_G + 2 * CT
G_NEXT = G_U + TT
GROUPS = G_NEXT + FILL
SPLITS = GROUPS - 2 * CT
STACK_INC = 6 * 16
V_INC = W_INC = 2 * 16

LAG0 = 2
STEPS0 = UNITS_PAIR + 7
FILL_STEPS = {3: 0, 6: 1, 9: 2, 12: 3, 16: 4, 17: 5}
PROJ_STEPS = {15: 0, 16: 1, 17: 2, 18: 3}
NEXT_STEPS = {4: 0, 5: 1, 6: 2, 7: 3, 8: 4, 9: 5}
STEPS1 = TT + 4


def group_count(b, m):
    return b * GROUPS + (FILL + m + 1)


def split_count(b, m):
    return b * SPLITS + (FILL + (m if m < G_PROJ0 else m - 2 * CT) + 1)


def unit_count(b, n):
    return b * UNITS + (n + 1)


def staged_pv(b, v):
    return b * PVS + (v + 2)


def used_pv(b, v):
    return b * PVS + (v + 3)


def pair_unit(u):
    return u % 2, 2 * (u // 4) + (u % 4) // 2


def build(nc, x, w, y, consts, scratch, scratch_b):
    ctx = ExitStack()
    with ctx:
        def sb(name, cols, dt=F32):
            return ctx.enter_context(nc.sbuf_tensor(name, [P, cols], dt))

        def sem(name):
            return ctx.enter_context(nc.semaphore(name))

        def f16(ap):
            return ap.bitcast(F16)

        xin = sb("xin", CT * T)
        r2 = sb("x1_att", 2 * CT * T)
        r1 = sb("probs_t", 8192)
        r3 = sb("stacks_probs", 8192)
        z0buf = sb("z0", CT * T)
        natbuf = sb("nat", 3072)
        globuf = sb("g_lo", 2048)
        stgbuf = sb("staging", 2 * HALF)
        pvsbuf = sb("pv_staging", 2 * HALF)
        zstbuf = sb("z_staging", 2 * T)
        wcurbuf = sb("wqkv_pair", 1538)
        wp0 = sb("wp0", 2 * CT * C, F16)
        wm1 = sb("wm1", 2 * CT * C, F16)
        wu1 = sb("wu1", 2 * CT * C, F16)
        cst = sb("ident_gavg", 2 * P)
        ident16 = sb("ident16", P, F16)
        vec = sb("vectors", 64)
        small = sb("small", 160)

        xin_v = xin[:, :].rearrange("p (c t) -> p c t", c=CT)
        x1 = r2[:, 0:CT * T].rearrange("p (c t) -> p c t", c=CT)
        att = f16(r2[:, CT * T:]).rearrange("p (s c t) -> p s c t", s=2, c=CT)
        z1 = att
        z0 = f16(z0buf[:, :]).rearrange("p (s c t) -> p s c t", s=2, c=CT)
        probs_t = f16(r1[:, :]).rearrange("p (k h s j t) -> p k h s j t", k=2, h=2, s=2, j=TT)
        u_t = [f16(r1[:, 4096 * s + 2048:4096 * s + 4096]).rearrange("p (j o) -> p j o", j=TT) for s in range(2)]
        stacks = f16(r3[:, 0:3072]).rearrange("p (s h t) -> p s h t", s=3, h=2)
        v_cur = f16(r3[:, 3072:4096]).rearrange("p (s j c) -> p s j c", s=2, j=TT)
        probs32 = r3[:, 4096:6144].rearrange("p (k t) -> p k t", k=2)
        probs_hi = f16(r3[:, 6144:7168]).rearrange("p (k t) -> p k t", k=2)
        probs_lo = f16(r3[:, 7168:8192]).rearrange("p (k t) -> p k t", k=2)
        g_s = [f16(r3[:, 0:2048]).rearrange("p (c t) -> p c t", c=CT),
               f16(globuf[:, :]).rearrange("p (c t) -> p c t", c=CT)]
        qk_nat = f16(natbuf[:, 0:2048]).rearrange("p (n s t) -> p n s t", n=2, s=2)
        v_nat = f16(natbuf[:, 2048:3072]).rearrange("p (s j c) -> p s j c", s=2, j=TT)
        stg = stgbuf[:, :].rearrange("p (k t) -> p k t", k=2)
        pvs = pvsbuf[:, :].rearrange("p (k t) -> p k t", k=2)
        zst = zstbuf[:, :].rearrange("p (k t) -> p k t", k=2)
        w_cur = f16(wcurbuf[:, 0:1536]).rearrange("p (s c n o) -> p s c n o", s=2, c=CT, n=3)
        b_cur = wcurbuf[:, 1536:1538]
        wp0_v = wp0[:, :].rearrange("p (s c o) -> p s c o", s=2, c=CT)
        wm1_v = wm1[:, :].rearrange("p (s c o) -> p s c o", s=2, c=CT)
        wu1_v = wu1[:, :].rearrange("p (s c o) -> p s c o", s=2, c=CT)
        ident = cst[:, 0:P]
        gavg = cst[:, P:2 * P]

        w0t = r2[:, 0:6144].rearrange("p (c o) -> p c o", c=CT)
        wp0t = r2[:, 6144:8192].rearrange("p (c o) -> p c o", c=CT)
        wq1, wk1, wv1 = (r3[:, 2048 * i:2048 * i + 2048].rearrange("p (j c) -> p j c", j=CT) for i in range(3))
        m_raw = z0buf[:, 0:2048].rearrange("p (c o) -> p c o", c=CT)
        u_raw = z0buf[:, 2048:4096].rearrange("p (c o) -> p c o", c=CT)
        wp1t = globuf[:, :].rearrange("p (c o) -> p c o", c=CT)
        gain_row = stgbuf[:, 0:C]
        w0s = [f16(r1[:, 3072 * s:3072 * s + 3072]).rearrange("p (c n j o) -> p c n j o", c=CT, n=3, j=PAIRS)
               for s in range(2)]

        gain0, shift0 = vec[:, 0:4], vec[:, 4:8]
        bqkv, bp0_in = vec[:, 8:20], vec[:, 20:24]
        gain1, shift1 = vec[:, 24:28], vec[:, 28:32]
        bq1, bv1, bp1_in = vec[:, 32:36], vec[:, 36:40], vec[:, 40:44]
        b_qkv = small[:, 0:12]
        b_g = small[:, 12:16]
        b_out1 = small[:, 16:20]
        b_out0 = small[:, 20:24]
        tops = small[:, 24:28]
        inv = small[:, 28:32]
        exp_scale = small[:, 32:34]
        out_scale = small[:, 34:36]
        b_qk = small[:, 36:44].rearrange("p (n j) -> p n j", n=2)
        tmp = small[:, 52:76]
        neg_half = small[:, 76:80]
        neg_max = small[:, 80:82]
        exp_bias = small[:, 82:84]
        row_sum = small[:, 84:86]
        row_inv = small[:, 86:88]
        row_scaled = small[:, 88:90]
        gn_stats = sb("gn_stats", CT * 12)
        gn = small[:, 96:144].rearrange("p (k c) -> p k c", c=CT)
        gn_sub = sb("gn_sub", 4 * CT)
        gn_parts = gn_stats[:, :].rearrange("p (c s k) -> p c s k", c=CT, s=4)

        scores = ctx.enter_context(nc.psum_tensor("scores", [P, 2, 2, HALF], F32))
        trans = ctx.enter_context(nc.psum_tensor("transposed", [P, 2, T], F16))
        pv = ctx.enter_context(nc.psum_tensor("pv", [P, HALF], F32))
        proj = ctx.enter_context(nc.psum_tensor("proj", [P, HALF], F32))

        loaded0, loaded1, loadedv = sem("loaded0"), sem("loaded1"), sem("loadedv")
        bank_filled, bank_read = sem("bank_filled"), sem("bank_read")
        bias_sums, bias0_ready, bias_proj = sem("bias_sums"), sem("bias0_ready"), sem("bias_proj")
        tops_in, tops_out = sem("tops_in"), sem("tops_out")
        setup_chain = sem("setup_chain")
        w0_split, w0_stored = sem("w0_split"), sem("w0_stored")
        pvs_full, pvs_used = sem("pvs_full"), sem("pvs_used")

        with nc.Block() as block:
            @block.sync
            def _(sp):
                for dst, name in ((wq1, "q1"), (wk1, "k1"), (wv1, "v1"), (wp1t, "p1_t")):
                    sp.dma_start(dst, w[name].rearrange("(j p) c -> p j c", p=P)).then_inc(loaded1, 16)
                sp.dma_start(vec[:, 0:44], w["vectors"]).then_inc(loadedv, 16)
                sp.dma_start(cst[:, :], consts).then_inc(loadedv, 16)
                sp.dma_start(gain_row, w["gain1"].rearrange("(a n) -> a n", a=1).broadcast_to([P, C])).then_inc(loadedv, 16)
                for dst, name in ((w0t, "qkv_t"), (wp0t, "p0_t")):
                    sp.dma_start(dst, w[name].rearrange("(j p) c -> p j c", p=P)).then_inc(loaded0, 16)
                sp.wait_ge(w0_split, 1)
                for s in range(2):
                    for p in range(PAIRS):
                        sp.dma_start(scratch[p, :, s * 1536:s * 1536 + 1536].rearrange("p (c n o) -> p c n o", c=CT, n=3),
                                     w0s[s][:, :, :, p, :]).then_inc(w0_stored, 16)
                for p in range(PAIRS):
                    sp.dma_start(scratch_b[p], b_qk[:, :, p], allow_slow_non_contiguous=True).then_inc(w0_stored, 16)
                sp.wait_ge(w0_stored, 3 * PAIRS * 16)

            @block.gpsimd
            def _(pool):
                nc.gpsimd.memset(neg_half, -0.5).then_inc(pvs_used, 2)
                pool.wait_ge(tops_in, 1)
                nc.gpsimd.partition_all_reduce(tops, tmp[:, 0:4], P, ABSMAX).then_inc(tops_out, 1)

            @block.tensor
            def _(pe):
                banks = [scores[:, k // 2, k % 2, :] for k in range(4)]
                fill = 0

                pe.wait_ge(loaded1, 4 * 16)
                for a_nat, b_v in ((wq1, wk1), (wv1, wp1t)):
                    for c in range(CT):
                        if fill >= 4:
                            pe.wait_ge(bank_read, fill - 3)
                        for k in range(CT):
                            last = nc.tensor.matmul(banks[fill % 4], a_nat[:, k, c * P:c * P + P], b_v[:, k, :],
                                                    start=(k == 0), stop=(k == CT - 1))
                        last.then_inc(bank_filled, 1)
                        fill += 1
                pe.wait_ge(loadedv, 3 * 16)
                pe.wait_ge(loaded0, 2 * 16)
                pe.wait_ge(bank_read, 2 * CT)
                for o in range(12):
                    for c in range(CT):
                        nc.tensor.matmul(proj[:, o:o + 1], w0t[:, c, o * P:o * P + P], shift0[:, c:c + 1],
                                         start=(c == 0), stop=(c == CT - 1))
                for o in range(CT):
                    cols = slice(o * P, o * P + P)
                    for k, (a, v) in enumerate([(m_raw, shift1), (wk1, bq1)]):
                        for c in range(CT):
                            nc.tensor.matmul(proj[:, 12 + o:13 + o], a[:, c, cols], v[:, c:c + 1],
                                             start=(k + c == 0), stop=(k == 1 and c == CT - 1))
                for o in range(CT):
                    cols = slice(o * P, o * P + P)
                    for k, (a, v) in enumerate([(u_raw, shift1), (wp1t, bv1)]):
                        for c in range(CT):
                            last = nc.tensor.matmul(proj[:, 16 + o:17 + o], a[:, c, cols], v[:, c:c + 1],
                                                    start=(k + c == 0), stop=(k == 1 and c == CT - 1))
                last.then_inc(bias_sums, 1)
                pe.wait_ge(bias0_ready, 1)
                for o in range(CT):
                    for c in range(CT):
                        last = nc.tensor.matmul(pv[:, o:o + 1], wp0t[:, c, o * P:o * P + P], b_qkv[:, 8 + c:9 + c],
                                                start=(c == 0), stop=(c == CT - 1))
                last.then_inc(bias_proj, 1)

            @block.scalar
            def _(act):
                banks = [scores[:, k // 2, k % 2, :] for k in range(4)]
                for n, d in enumerate([raw[:, c, :] for raw in (m_raw, u_raw) for c in range(CT)]):
                    act.wait_ge(bank_filled, n + 1)
                    nc.scalar.activation(d, banks[n % 4], ACT.Copy).then_inc(bank_read, 1)
                act.wait_ge(loadedv, 3 * 16)
                nc.scalar.activation(ident16[:, :], ident, ACT.Copy).then_inc(pvs_full, 1)

            @block.vector
            def _(dve):
                chain = 0

                def step(ins):
                    nonlocal chain
                    chain += 1
                    ins.then_inc(setup_chain, 1)
                    dve.wait_ge(setup_chain, chain)

                v = nc.vector
                dve.wait_ge(loadedv, 3 * 16)
                dve.wait_ge(bias_sums, 1)
                v.tensor_tensor(b_qkv, proj[:, 0:12], bqkv, ALU.add).then_inc(bias0_ready, 1)
                dve.wait_ge(bias0_ready, 1)
                step(v.tensor_tensor(b_g, proj[:, 12:16], gain1, ALU.mult))
                step(v.tensor_tensor(b_out1, proj[:, 16:20], bp1_in, ALU.add))
                for c in range(CT):
                    step(v.tensor_scalar(m_raw[:, c, :], m_raw[:, c, :], gain1[:, c:c + 1], None, ALU.mult))
                    step(v.tensor_tensor(m_raw[:, c, :], m_raw[:, c, :], gain_row, ALU.mult))
                    step(v.tensor_scalar(u_raw[:, c, :], u_raw[:, c, :], gain1[:, c:c + 1], None, ALU.mult))
                for c in range(CT):
                    step(v.tensor_reduce(tmp[:, 8 + c:9 + c], w0t[:, c, :], AX.X, ALU.max, apply_absolute_value=True))
                step(v.tensor_tensor(tmp[:, 8:12], tmp[:, 8:12], gain0, ALU.mult))
                step(v.tensor_reduce(tmp[:, 0:1], tmp[:, 8:12], AX.X, ALU.max, apply_absolute_value=True))
                step(v.tensor_reduce(tmp[:, 4:5], b_qkv, AX.X, ALU.max, apply_absolute_value=True))
                step(v.tensor_reduce(tmp[:, 1:2], wp0t, AX.XY, ALU.max, apply_absolute_value=True))
                step(v.tensor_reduce(tmp[:, 2:3], m_raw, AX.XY, ALU.max, apply_absolute_value=True))
                step(v.tensor_reduce(tmp[:, 5:6], b_g, AX.X, ALU.max, apply_absolute_value=True))
                step(v.tensor_reduce(tmp[:, 3:4], u_raw, AX.XY, ALU.max, apply_absolute_value=True))
                step(v.tensor_tensor(tmp[:, 0:1], tmp[:, 0:1], tmp[:, 4:5], ALU.max))
                v.tensor_tensor(tmp[:, 2:3], tmp[:, 2:3], tmp[:, 5:6], ALU.max).then_inc(tops_in, 1)
                dve.wait_ge(tops_out, 1)
                step(v.tensor_scalar(tops, tops, 1e-30, None, ALU.max))
                step(v.reciprocal(inv, tops))
                step(v.tensor_scalar(tmp[:, 0:4], inv, 0.5, None, ALU.mult))
                step(v.tensor_scalar(small[:, 36:44], b_qkv[:, 0:8], tmp[:, 0:1], None, ALU.mult))
                step(v.tensor_scalar(b_g, b_g, tmp[:, 2:3], None, ALU.mult))
                dve.wait_ge(bias_proj, 1)
                step(v.tensor_tensor(b_out0, pv[:, 0:4], bp0_in, ALU.add))
                step(v.tensor_tensor(tmp[:, 4:5], tops[:, 0:1], tops[:, 0:1], ALU.mult))
                step(v.tensor_scalar(exp_scale[:, 0:1], tmp[:, 4:5], 4.0 / CH ** 0.5, None, ALU.mult))
                step(v.tensor_scalar(exp_scale[:, 1:2], tops[:, 2:3], 2.0 / (ZSC * C ** 0.5), None, ALU.mult))
                step(v.tensor_tensor(tmp[:, 5:6], tops[:, 0:1], tops[:, 1:2], ALU.mult))
                step(v.tensor_scalar(out_scale[:, 0:1], tmp[:, 5:6], 2.0 / WSC, None, ALU.mult))
                step(v.tensor_scalar(out_scale[:, 1:2], tops[:, 3:4], 2.0 / PSC, None, ALU.mult))
                step(v.tensor_scalar(inv, inv, WSC, None, ALU.mult))
                step(v.tensor_scalar(tmp[:, 0:4], gain0, inv[:, 0:1], None, ALU.mult))
                for c in range(CT):
                    step(v.tensor_scalar(w0t[:, c, :], w0t[:, c, :], tmp[:, c:c + 1], None, ALU.mult))
                step(v.tensor_copy(w0s[0].rearrange("p c n j o -> p (c n j o)"), w0t.rearrange("p c o -> p (c o)")))
                v.tensor_tensor(w0s[1].rearrange("p c n j o -> p (c n j o)"), w0t.rearrange("p c o -> p (c o)"),
                                w0s[0].rearrange("p c n j o -> p (c n j o)"), ALU.subtract).then_inc(w0_split, 1)
                for k, (raw, pair) in enumerate(((wp0t, wp0_v), (m_raw, wm1_v), (u_raw, wu1_v))):
                    step(v.tensor_scalar(raw, raw, inv[:, k + 1:k + 2], None, ALU.mult))
                    step(v.tensor_copy(pair[:, 0], raw))
                    step(v.tensor_tensor(pair[:, 1], raw, pair[:, 0], ALU.subtract))

        x_loaded, y_stored = sem("x_loaded"), sem("y_stored")
        w_loaded = sem("w_loaded")
        stack_a, stack_b, v_moved = sem("stack_a"), sem("stack_b"), sem("v_moved")
        scores_done, neg_max_done, bias_done = sem("scores_done"), sem("neg_max_done"), sem("bias_done")
        exp_done, sum_scaled, inv_done = sem("exp_done"), sem("sum_scaled"), sem("inv_done")
        hi_done, lo_done = sem("hi_done"), sem("lo_done")
        trans_hi, trans_lo = sem("trans_hi"), sem("trans_lo")
        kept_hi, kept_lo = sem("kept_hi"), sem("kept_lo")
        pv_done, pvs_hi = sem("pv_done"), sem("pvs_hi")
        group_done, stg_full, stg_hi, stg_used = sem("group_done"), sem("stg_full"), sem("stg_hi"), sem("stg_used")
        gn_in, gn_out, gn_chain = sem("gn_in"), sem("gn_out"), sem("gn_chain")
        pow_in, pow_out, z_coef = sem("pow_in"), sem("pow_out"), sem("z_coef")
        z32_done, z_hi, z_done = sem("z32_done"), sem("z_hi"), sem("z_done")
        GN_CHAIN = 10

        def per_batch(eng, body):
            with eng.Fori(0, B - 1) as b:
                body(b, False)
            body(B - 1, True)

        def per_pair(eng, b, body):
            with eng.Fori(0, PAIRS - 1) as p:
                body(p, False)
            body(PAIRS - 1, True)

        with nc.Block() as block:
            @block.sync
            def _(sp):
                def stacks_of(head, done):
                    rows = slice(head * CH, head * CH + CH)
                    low, high = slice(0, CH), slice(CH, P)
                    q_hi, q_lo = qk_nat[rows, 0, 0, :], qk_nat[rows, 0, 1, :]
                    k_hi, k_lo = qk_nat[rows, 1, 0, :], qk_nat[rows, 1, 1, :]
                    for dst, src in ((stacks[low, 0, head], q_hi), (stacks[high, 0, head], q_lo),
                                     (stacks[low, 2, head], k_hi), (stacks[high, 2, head], k_lo),
                                     (stacks[low, 1, head], q_lo), (stacks[high, 1, head], q_hi)):
                        sp.dma_start(dst, src).then_inc(done, 16)

                def move_v(*halves):
                    for s in halves:
                        sp.dma_start(v_cur[:, s], v_nat[:, s]).then_inc(v_moved, 16)

                def load_x(b):
                    sp.dma_start(xin_v, x[b].rearrange("(c p) t -> p c t", p=P)).then_inc(x_loaded, 16)

                def load_w(p):
                    sp.dma_start(f16(wcurbuf[:, 0:1536]), scratch[p]).then_inc(w_loaded, 16)
                    sp.dma_start(b_cur, scratch_b[p]).then_inc(w_loaded, 16)

                load_x(0)
                load_w(0)
                sp.wait_ge(stg_used, 4)
                stacks_of(0, stack_a)
                stacks_of(1, stack_b)
                sp.wait_ge(stg_used, FILL)
                move_v(0, 1)

                def batch(b, last):
                    def pair(p, last_pair):
                        bp = b * UNITS + p * UNITS_PAIR
                        if not last_pair:
                            sp.wait_ge(group_done, b * GROUPS + p * FILL + FILL)
                            load_w(p + 1)
                            sp.wait_ge(stg_used, b * GROUPS + p * FILL + (FILL + 4))
                            sp.wait_ge(scores_done, bp + UNITS_PAIR - 1)
                            stacks_of(0, stack_a)
                            sp.wait_ge(scores_done, bp + UNITS_PAIR)
                            stacks_of(1, stack_b)
                            sp.wait_ge(stg_used, b * GROUPS + p * FILL + 2 * FILL)
                            sp.wait_ge(pv_done, b * PVS + p * PV_PAIR + PV_PAIR)
                            move_v(0, 1)
                        elif not last:
                            sp.wait_ge(group_done, group_count(b, G_PROJ0 - 1))
                            load_w(0)

                    per_pair(sp, b, pair)
                    if not last:
                        sp.wait_ge(stg_used, group_count(b, G_G - 1))
                        load_x(b + 1)
                    for q in range(QUARTERS):
                        if q == 2 and not last:
                            sp.wait_ge(stg_used, group_count(b, G_NEXT + 3))
                            sp.wait_ge(scores_done, unit_count(b, UNITS - 1))
                            stacks_of(0, stack_a)
                            stacks_of(1, stack_b)
                        sp.wait_ge(pvs_used, used_pv(b, PV0 + 2 * q + 1))
                        cols = slice(256 * q, 256 * q + 256)
                        sp.dma_start(y[b].rearrange("(c p) t -> p c t", p=P)[:, :, cols], x1[:, :, cols])\
                          .then_inc(y_stored, 16)
                    if not last:
                        sp.wait_ge(stg_used, group_count(b, G_NEXT + 5))
                        move_v(0)
                    sp.wait_ge(y_stored, (b * QUARTERS + QUARTERS) * 16)
                    if not last:
                        move_v(1)

                per_batch(sp, batch)

            @block.tensor
            def _(pe):
                THREE = ((0, 0), (0, 1), (1, 0))

                def group(out, terms):
                    n = 3 * len(terms)
                    k = 0
                    for lhs, rhs in terms:
                        for a, c in THREE:
                            last = nc.tensor.matmul(out, lhs(a), rhs(c), start=(k == 0), stop=(k == n - 1))
                            k += 1
                    return last

                def qkv_group(j):
                    if j < 4:
                        n, cols = (1, 0)[j // 2], slice((j % 2) * HALF, (j % 2) * HALF + HALF)
                        return group(proj[:, :], [(lambda s, c=c: w_cur[:, s, c, n, :], lambda s, c=c: z0[:, s, c, cols])
                                                  for c in range(CT)])
                    for i in range(4):
                        rows = slice((4 * (j - 4) + i) * P, (4 * (j - 4) + i) * P + P)
                        last = group(proj[:, i * P:i * P + P],
                                     [(lambda s, c=c: z0[:, s, c, rows], lambda s, c=c: w_cur[:, s, c, 2, :])
                                      for c in range(CT)])
                    return last

                def transposes(n, par):
                    for s, (ready, done) in enumerate(((hi_done, trans_hi), (lo_done, trans_lo))):
                        src = (probs_hi, probs_lo)[s]
                        pe.wait_ge(ready, n)
                        for j in range(TT):
                            last = nc.tensor.transpose(trans[:, s, j * P:j * P + P], src[:, par, j * P:j * P + P],
                                                       ident16[:, :])
                        last.then_inc(done, 1)

                def gn_sums(n):
                    for k in range(2):
                        pe.wait_ge(gn_in, 2 * n + (k + 1))
                        nc.tensor.matmul(proj[:, k * CT:k * CT + CT], gavg,
                                         gn[:, 0, :] if k == 0 else gn[:, 3, :],
                                         start=True, stop=True).then_inc(gn_out, 1)

                gn_sums(0)
                pe.wait_ge(z_done, CT)
                pe.wait_ge(w_loaded, W_INC)
                for j in range(FILL):
                    if j:
                        pe.wait_ge(stg_full, j)
                    qkv_group(j).then_inc(group_done, 1)

                def batch(b, last):
                    def pair(p, last_pair):
                        n0 = b * UNITS + p * UNITS_PAIR
                        v0 = b * PVS + p * PV_PAIR
                        m0 = b * GROUPS + p * FILL + FILL
                        moved = b * PAIRS + p + 1
                        for st in range(STEPS0):
                            if st < UNITS_PAIR:
                                head, tile = pair_unit(st)
                                if st < 2:
                                    pe.wait_ge((stack_a, stack_b)[st], moved * STACK_INC)
                                else:
                                    pe.wait_ge(exp_done, n0 + st - 1)
                                for half in range(2):
                                    cols = slice(half * HALF, half * HALF + HALF)
                                    for k in range(2):
                                        mm = nc.tensor.matmul(scores[:, st % 2, half, :],
                                                              stacks[:, k, head, tile * P:tile * P + P],
                                                              stacks[:, 2, head, cols], start=(k == 0), stop=(k == 1))
                                mm.then_inc(scores_done, 1)
                            if not last_pair and st in FILL_STEPS:
                                j = FILL_STEPS[st]
                                if j == 0:
                                    pe.wait_ge(w_loaded, (b * PAIRS + p + 2) * W_INC)
                                pe.wait_ge(stg_full, m0 + j)
                                qkv_group(j).then_inc(group_done, 1)
                            if last_pair and st in PROJ_STEPS:
                                o = PROJ_STEPS[st]
                                if o == 0:
                                    pe.wait_ge(pvs_used, used_pv(b, p * PV_PAIR + 1))
                                pe.wait_ge(stg_full, group_count(b, G_PROJ0 + o - 1))
                                out_proj(o, 0, proj).then_inc(group_done, 1)
                            u = st - LAG0
                            if 0 <= u < UNITS_PAIR:
                                if u:
                                    pe.wait_ge(kept_hi, n0 + u)
                                    pe.wait_ge(kept_lo, n0 + u)
                                transposes(n0 + (u + 1), u % 2)
                            for q in range(QUARTERS):
                                j = st - (4 * q + 6)
                                if 0 <= j < 4:
                                    if j == 0:
                                        pe.wait_ge(kept_hi, n0 + 4 * q + 4)
                                        pe.wait_ge(kept_lo, n0 + 4 * q + 4)
                                        pe.wait_ge(pvs_full, v0 + q + 1)
                                        if q == 0:
                                            pe.wait_ge(v_moved, moved * V_INC)
                                    for kt in (2 * j, 2 * j + 1):
                                        for i, (a, c) in enumerate(THREE):
                                            for head in range(2):
                                                mm = nc.tensor.matmul(
                                                    pv[head * CH:head * CH + CH, 0:256],
                                                    v_cur[:, a, kt, head * CH:head * CH + CH],
                                                    probs_t[:, q % 2, head, c, kt, :],
                                                    start=(kt == 0 and i == 0), stop=(kt == TT - 1 and i == 2))
                                    if j == 3:
                                        mm.then_inc(pv_done, 1)

                    def out_proj(o, half, bank):
                        cols = slice(half * HALF, half * HALF + HALF)
                        return group(bank[:, :], [(lambda s, c=c: wp0_v[:, s, c, o * P:o * P + P],
                                                   lambda s, c=c: att[:, s, c, cols]) for c in range(CT)])

                    per_pair(pe, b, pair)

                    banks = (proj, pv)
                    for o in range(CT):
                        if o == 0:
                            pe.wait_ge(pvs_used, used_pv(b, PV0 - 1))
                        pe.wait_ge(stg_full, group_count(b, G_PROJ1 + o - (1 if o == 0 else 2)))
                        out_proj(o, 1, banks[o % 2]).then_inc(group_done, 1)
                    pe.wait_ge(stg_full, group_count(b, G_G - 1))
                    gn_sums(b * 2 + 1)
                    pe.wait_ge(z_done, (b * 2 + 2) * CT)
                    for m in range(2 * CT):
                        half, o = m // CT, m % CT
                        cols = slice(half * HALF, half * HALF + HALF)
                        pe.wait_ge(stg_full, group_count(b, G_G + m - 2))
                        group(banks[m % 2][:, :], [(lambda s, c=c: wm1_v[:, s, c, o * P:o * P + P],
                                                    lambda s, c=c: z1[:, s, c, cols]) for c in range(CT)])\
                            .then_inc(group_done, 1)
                    for m in range(TT):
                        pe.wait_ge(stg_full, group_count(b, G_U + m - 2))
                        group(banks[m % 2][:, :], [(lambda s, c=c: z1[:, s, c, m * P:m * P + P],
                                                    lambda s, c=c: wu1_v[:, s, c, :]) for c in range(CT)])\
                            .then_inc(group_done, 1)

                    n0 = b * UNITS + UNITS0
                    v0 = b * PVS + PV0
                    for st in range(STEPS1 - 1):
                        if st < TT:
                            if st == 0:
                                pe.wait_ge(stg_used, group_count(b, G_U - 1))
                            if st >= 2:
                                pe.wait_ge(exp_done, n0 + st - 1)
                            for half in range(2):
                                cols = slice(half * HALF, half * HALF + HALF)
                                mm = group(scores[:, st % 2, half, :],
                                           [(lambda s, c=c: g_s[s][:, c, st * P:st * P + P],
                                             lambda s, c=c: z1[:, s, c, cols]) for c in range(CT)])
                            mm.then_inc(scores_done, 1)
                        if not last and st == 3:
                            pe.wait_ge(stg_full, group_count(b, G_NEXT - 1))
                            gn_sums(b * 2 + 2)
                        if not last and st in NEXT_STEPS:
                            j = NEXT_STEPS[st]
                            if j == 0:
                                pe.wait_ge(z_done, (b * 2 + 3) * CT)
                                pe.wait_ge(w_loaded, (b * PAIRS + PAIRS + 1) * W_INC)
                            else:
                                pe.wait_ge(stg_full, group_count(b, G_NEXT + j - 1))
                            qkv_group(j).then_inc(group_done, 1)
                        for q in range(QUARTERS):
                            for k in range(2):
                                if st == 2 * q + 3 + k:
                                    if k == 0:
                                        pe.wait_ge(kept_hi, n0 + 2 * q + 2)
                                        pe.wait_ge(kept_lo, n0 + 2 * q + 2)
                                    if q == 0 and k == 0:
                                        pe.wait_ge(stg_used, group_count(b, G_NEXT - 1))
                                    pe.wait_ge(pvs_full, v0 + 2 * q + k + 1)
                                    for i in range(2):
                                        o = 2 * k + i
                                        mm = group(pv[:, 256 * i:256 * i + 256],
                                                   [(lambda s, kt=kt: u_t[s][:, kt, o * P:o * P + P],
                                                     lambda s, kt=kt: probs_t[:, q % 2, 0, s, kt, :])
                                                    for kt in range(TT)])
                                    mm.then_inc(pv_done, 1)
                        u = st - 1
                        if 0 <= u < TT:
                            if u:
                                pe.wait_ge(kept_hi, n0 + u)
                                pe.wait_ge(kept_lo, n0 + u)
                            transposes(n0 + (u + 1), u % 2)

                per_batch(pe, batch)

            @block.scalar
            def _(act):
                def exponentials(n, par, layer, first):
                    act.wait_ge(bias_done, n)
                    if not first:
                        act.wait_ge(lo_done, n - 2)
                    nc.scalar.activation(probs32[:, par, :], scores[:, par, :, :].rearrange("p a t -> p (a t)"), ACT.Exp,
                                         bias=exp_bias[:, par:par + 1], scale=exp_scale[:, layer:layer + 1],
                                         accum_out=row_sum[:, par:par + 1]).then_inc(exp_done, 1)

                def keep(n, dst, free):
                    for s, (ready, done) in enumerate(((trans_hi, kept_hi), (trans_lo, kept_lo))):
                        act.wait_ge(ready, n)
                        if free is not None and s == 0:
                            act.wait_ge(pv_done, free)
                        nc.scalar.activation(dst[s], trans[:, s, :].rearrange("p (j t) -> p j t", j=TT), ACT.Copy)\
                          .then_inc(done, 1)

                def stage(count, m, src, scale, bias, two_back=True):
                    act.wait_ge(group_done, count)
                    if two_back:
                        act.wait_ge(stg_used, count - 2)
                    if bias is None:
                        nc.scalar.activation(stg[:, m % 2, :], src, ACT.Copy, scale=scale).then_inc(stg_full, 1)
                    else:
                        nc.scalar.activation(stg[:, m % 2, :], src, ACT.Identity, scale=scale, bias=bias)\
                          .then_inc(stg_full, 1)

                def qkv_stage(count, j, two_back=True):
                    n = (1, 0)[j // 2] if j < 4 else None
                    bias = None if n is None else b_cur[:, n:n + 1]
                    stage(count, j, proj[:, :], QSC, bias, two_back)

                def normalise(src, count):
                    act.wait_ge(z_coef, count)
                    for c in range(CT):
                        i = (count - 1) * CT + c
                        if c >= 2:
                            act.wait_ge(z_done, i - 1)
                        nc.scalar.activation(zst[:, c % 2, :], src[:, c, :], ACT.Identity,
                                             scale=gn[:, 8, c:c + 1], bias=gn[:, 9, c:c + 1]).then_inc(z32_done, 1)

                act.wait_ge(x_loaded, 16)
                normalise(xin_v, 1)
                for j in range(FILL):
                    qkv_stage(j + 1, j, two_back=j >= 2)

                def batch(b, last):
                    def pair(p, last_pair):
                        n0 = b * UNITS + p * UNITS_PAIR
                        v0 = b * PVS + p * PV_PAIR
                        m0 = b * GROUPS + p * FILL + FILL
                        for st in range(STEPS0):
                            if st < UNITS_PAIR:
                                exponentials(n0 + (st + 1), st % 2, 0, first=st < 2)
                            if not last_pair and st in FILL_STEPS:
                                j = FILL_STEPS[st]
                                qkv_stage(m0 + (j + 1), j)
                            if last_pair and st in PROJ_STEPS:
                                o = PROJ_STEPS[st]
                                stage(group_count(b, G_PROJ0 + o), o, proj[:, :], out_scale[:, 0:1], b_out0[:, o:o + 1])
                            u = st - LAG0
                            if 0 <= u < UNITS_PAIR:
                                head, tile = pair_unit(u)
                                q = u // 4
                                cols = slice((tile % 2) * P, (tile % 2) * P + P)
                                keep(n0 + (u + 1), [probs_t[:, q % 2, head, s, :, cols] for s in range(2)],
                                     v0 + (q - 1) if q >= 2 and u % 4 == 0 else None)
                            for q in range(QUARTERS):
                                if st == 4 * q + 9:
                                    act.wait_ge(pv_done, v0 + (q + 1))
                                    act.wait_ge(pvs_used, v0 + (q + 1))
                                    nc.scalar.activation(pvs[:, q % 2, 0:256], pv[:, 0:256], ACT.Copy, scale=1.0 / PSC)\
                                      .then_inc(pvs_full, 1)

                    per_pair(act, b, pair)
                    banks = (proj, pv)
                    for o in range(CT):
                        stage(group_count(b, G_PROJ1 + o), o, banks[o % 2][:, :], out_scale[:, 0:1], b_out0[:, o:o + 1])
                    normalise(x1, b * 2 + 2)
                    for m in range(2 * CT):
                        stage(group_count(b, G_G + m), m, banks[m % 2][:, :], QSC, b_g[:, m % CT:m % CT + 1])
                    for m in range(TT):
                        stage(group_count(b, G_U + m), m, banks[m % 2][:, :], QSC, None)
                    n0 = b * UNITS + UNITS0
                    v0 = b * PVS + PV0
                    for st in range(STEPS1):
                        if st < TT:
                            exponentials(n0 + (st + 1), st % 2, 1, first=st < 2)
                        if not last and st == 3:
                            normalise(xin_v, b * 2 + 3)
                        if not last and st in NEXT_STEPS:
                            j = NEXT_STEPS[st]
                            qkv_stage(group_count(b, G_NEXT + j), j)
                        for q in range(QUARTERS):
                            for k in range(2):
                                if st == 2 * q + 3 + k:
                                    act.wait_ge(pv_done, v0 + (2 * q + k + 1))
                                    act.wait_ge(pvs_used, v0 + (2 * q + k + 1))
                                    for i in range(2):
                                        o = 2 * k + i
                                        cp = nc.scalar.activation(pvs[:, k, 256 * i:256 * i + 256],
                                                                  pv[:, 256 * i:256 * i + 256], ACT.Identity,
                                                                  scale=out_scale[:, 1:2], bias=b_out1[:, o:o + 1])
                                    cp.then_inc(pvs_full, 1)
                        u = st - 1
                        if 0 <= u < TT:
                            q = u // 2
                            cols = slice((u % 2) * P, (u % 2) * P + P)
                            keep(n0 + (u + 1), [probs_t[:, q % 2, 0, s, :, cols] for s in range(2)],
                                 v0 + 2 * (q - 1) if q >= 2 and u % 2 == 0 else None)

                per_batch(act, batch)

            @block.vector
            def _(dve):
                v = nc.vector

                def row_max(n, par, layer):
                    dve.wait_ge(scores_done, n)
                    v.tensor_reduce(neg_max[:, par:par + 1], scores[:, par, :, :], AX.XY, ALU.max, negate=True)\
                     .then_inc(neg_max_done, 1)
                    dve.wait_ge(neg_max_done, n)
                    v.tensor_scalar(exp_bias[:, par:par + 1], neg_max[:, par:par + 1], exp_scale[:, layer:layer + 1],
                                    None, ALU.mult).then_inc(bias_done, 1)

                def split(n, par, first):
                    dve.wait_ge(exp_done, n)
                    v.tensor_scalar(row_scaled[:, par:par + 1], row_sum[:, par:par + 1], 1.0 / PSC, None, ALU.mult)\
                     .then_inc(sum_scaled, 1)
                    dve.wait_ge(sum_scaled, n)
                    v.reciprocal(row_inv[:, par:par + 1], row_scaled[:, par:par + 1]).then_inc(inv_done, 1)
                    dve.wait_ge(inv_done, n)
                    if not first:
                        dve.wait_ge(trans_lo, n - 2)
                    v.tensor_scalar(probs_hi[:, par, :], probs32[:, par, :], row_inv[:, par:par + 1], None, ALU.mult)\
                     .then_inc(hi_done, 1)
                    dve.wait_ge(hi_done, n)
                    v.scalar_tensor_tensor(probs_lo[:, par, :], probs32[:, par, :], row_inv[:, par:par + 1],
                                           probs_hi[:, par, :], ALU.mult, ALU.subtract).then_inc(lo_done, 1)

                def group_hi(dst, m, count):
                    dve.wait_ge(stg_full, count)
                    v.tensor_copy(dst, stg[:, m % 2, :]).then_inc(stg_hi, 1)

                def qkv_hi(j, count):
                    if j < 4:
                        cols = slice((j % 2) * HALF, (j % 2) * HALF + HALF)
                        group_hi(qk_nat[:, (1, 0)[j // 2], 0, cols], j, count)
                    else:
                        group_hi(v_nat[:, 0, 4 * (j - 4):4 * (j - 4) + 4, :].rearrange("p j c -> p (j c)"), j, count)

                def stats(src, c, half):
                    v.bn_stats(gn_stats[:, c * 12 + half * 6:c * 12 + half * 6 + 6],
                               src[:, c, half * HALF:half * HALF + HALF]).then_inc(gn_chain, 1)

                def norm_coefficients(k, eps):
                    base = k * (8 + GN_CHAIN)
                    done = [8]

                    def step(ins):
                        done[0] += 1
                        ins.then_inc(gn_chain, 1)
                        dve.wait_ge(gn_chain, base + done[0])

                    part_mean, part_sq = gn_parts[:, :, :, 1], gn_parts[:, :, :, 2]
                    d = gn_sub[:, :].rearrange("p (c s) -> p c s", c=CT)
                    g_mean, spread, e, r, t = (gn[:, i, :] for i in (2, 3, 4, 5, 6))
                    dve.wait_ge(gn_chain, base + 8)
                    v.tensor_reduce(gn[:, 0, :], part_mean, AX.X, ALU.add).then_inc(gn_in, 1)
                    dve.wait_ge(gn_out, 2 * k + 1)
                    step(v.tensor_scalar(g_mean, proj[:, 0:CT], 0.25, None, ALU.mult))
                    for c in range(CT):
                        ins = v.tensor_scalar(d[:, c, :], part_mean[:, c, :], g_mean[:, c:c + 1], None, ALU.subtract)
                    step(ins)
                    step(v.tensor_tensor(d, d, d, ALU.mult))
                    step(v.scalar_tensor_tensor(d, d, T / 4.0, part_sq, ALU.mult, ALU.add))
                    v.tensor_reduce(spread, d, AX.X, ALU.add).then_inc(gn_in, 1)
                    dve.wait_ge(gn_out, 2 * k + 2)
                    v.tensor_scalar(e, proj[:, CT:2 * CT], 1.0 / T, eps, ALU.mult, ALU.add).then_inc(pow_in, 1)
                    dve.wait_ge(pow_out, k + 1)
                    step(v.tensor_tensor(t, r, r, ALU.mult))
                    step(v.tensor_tensor(t, t, e, ALU.mult))
                    step(v.tensor_scalar(t, t, -0.5, 1.5, ALU.mult, ALU.add))
                    step(v.tensor_tensor(t, t, r, ALU.mult))
                    step(v.tensor_scalar(gn[:, 8, :], t, ZSC, None, ALU.mult))
                    step(v.tensor_tensor(t, g_mean, gn[:, 8, :], ALU.mult))
                    v.tensor_scalar(gn[:, 9, :], t, -1.0, None, ALU.mult).then_inc(z_coef, 1)
                    assert done[0] == 8 + GN_CHAIN

                def norm_split(dst, k):
                    for c in range(CT):
                        dve.wait_ge(z32_done, k * CT + (c + 1))
                        v.tensor_copy(dst[:, 0, c, :], zst[:, c % 2, :]).then_inc(z_hi, 1)
                        dve.wait_ge(z_hi, k * CT + (c + 1))
                        v.tensor_tensor(dst[:, 1, c, :], zst[:, c % 2, :], dst[:, 0, c, :], ALU.subtract)\
                         .then_inc(z_done, 1)

                def all_stats(src):
                    for c in range(CT):
                        for half in range(2):
                            stats(src, c, half)

                dve.wait_ge(x_loaded, 16)
                all_stats(xin_v)
                norm_coefficients(0, EPS0)
                norm_split(z0, 0)
                for j in range(FILL):
                    qkv_hi(j, j + 1)

                def batch(b, last):
                    def pair(p, last_pair):
                        n0 = b * UNITS + p * UNITS_PAIR
                        v0 = b * PVS + p * PV_PAIR
                        m0 = b * GROUPS + p * FILL + FILL
                        for st in range(STEPS0):
                            if st < UNITS_PAIR:
                                row_max(n0 + (st + 1), st % 2, 0)
                            u = st - 1
                            if 0 <= u < UNITS_PAIR:
                                split(n0 + (u + 1), u % 2, first=u < 2)
                            if not last_pair and st in FILL_STEPS:
                                j = FILL_STEPS[st]
                                qkv_hi(j, m0 + (j + 1))
                            for q in range(QUARTERS):
                                if st == 4 * q + 10:
                                    dve.wait_ge(pvs_full, v0 + (q + 2))
                                    v.tensor_copy(att[:, 0, bass.ds(p, 1), 256 * q:256 * q + 256].rearrange("p a t -> p (a t)")
                                                  if not isinstance(p, int) else att[:, 0, p, 256 * q:256 * q + 256],
                                                  pvs[:, q % 2, 0:256]).then_inc(pvs_hi, 1)

                    per_pair(dve, b, pair)
                    for half in range(2):
                        for c in range(CT):
                            dve.wait_ge(stg_used, group_count(b, (G_PROJ0, G_PROJ1)[half] + c))
                            stats(x1, c, half)
                    norm_coefficients(b * 2 + 1, EPS1)
                    norm_split(z1, b * 2 + 1)
                    for m in range(2 * CT):
                        half, o = m // CT, m % CT
                        group_hi(g_s[0][:, o, half * HALF:half * HALF + HALF], m, group_count(b, G_G + m))
                    for m in range(TT):
                        group_hi(u_t[0][:, m, :], m, group_count(b, G_U + m))
                    n0 = b * UNITS + UNITS0
                    for st in range(STEPS1):
                        u = st - 1
                        if 0 <= u < TT:
                            split(n0 + (u + 1), u % 2, first=u < 2)
                        if st < TT:
                            row_max(n0 + (st + 1), st % 2, 1)
                        if not last and st == 2:
                            dve.wait_ge(x_loaded, (b + 2) * 16)
                            all_stats(xin_v)
                            norm_coefficients(b * 2 + 2, EPS0)
                        if not last and st == 3:
                            norm_split(z0, b * 2 + 2)
                        if not last and st in NEXT_STEPS:
                            j = NEXT_STEPS[st]
                            qkv_hi(j, group_count(b, G_NEXT + j))

                per_batch(dve, batch)

            @block.gpsimd
            def _(pool):
                g = nc.gpsimd

                def group_lo(lo, hi, m, count):
                    pool.wait_ge(stg_hi, count)
                    g.tensor_tensor(lo, stg[:, m % 2, :], hi, ALU.subtract).then_inc(stg_used, 1)

                def qkv_lo(j, count):
                    if j < 4:
                        n, cols = (1, 0)[j // 2], slice((j % 2) * HALF, (j % 2) * HALF + HALF)
                        group_lo(qk_nat[:, n, 1, cols], qk_nat[:, n, 0, cols], j, count)
                    else:
                        rows = slice(4 * (j - 4), 4 * (j - 4) + 4)
                        group_lo(v_nat[:, 1, rows, :].rearrange("p j c -> p (j c)"),
                                 v_nat[:, 0, rows, :].rearrange("p j c -> p (j c)"), j, count)

                def residual0(b, m, c, half):
                    pool.wait_ge(stg_full, group_count(b, m))
                    cols = slice(half * HALF, half * HALF + HALF)
                    g.tensor_tensor(x1[:, c, cols], stg[:, m % 2, :], xin_v[:, c, cols], ALU.add).then_inc(stg_used, 1)

                def rough_rsqrt(k):
                    pool.wait_ge(pow_in, k + 1)
                    g.tensor_tensor(gn[:, 5, :], gn[:, 4, :], neg_half, ALU.pow).then_inc(pow_out, 1)

                rough_rsqrt(0)
                for j in range(FILL):
                    qkv_lo(j, j + 1)

                def batch(b, last):
                    def pair(p, last_pair):
                        v0 = b * PVS + p * PV_PAIR
                        s0 = b * SPLITS + p * FILL + FILL
                        for st in range(STEPS0):
                            if not last_pair and st in FILL_STEPS:
                                j = FILL_STEPS[st]
                                qkv_lo(j, s0 + (j + 1))
                            if last_pair and st in PROJ_STEPS:
                                o = PROJ_STEPS[st]
                                residual0(b, G_PROJ0 + o, o, 0)
                            for q in range(QUARTERS):
                                if st == 4 * q + 10:
                                    cols = slice(256 * q, 256 * q + 256)
                                    at = [att[:, s, bass.ds(p, 1), cols].rearrange("p a t -> p (a t)")
                                          if not isinstance(p, int) else att[:, s, p, cols] for s in range(2)]
                                    pool.wait_ge(pvs_hi, b * PV0 + p * PV_PAIR + (q + 1))
                                    g.tensor_tensor(at[1], pvs[:, q % 2, 0:256], at[0], ALU.subtract)\
                                     .then_inc(pvs_used, 1)

                    per_pair(pool, b, pair)
                    for o in range(CT):
                        residual0(b, G_PROJ1 + o, o, 1)
                    rough_rsqrt(b * 2 + 1)
                    for m in range(2 * CT):
                        half, o = m // CT, m % CT
                        cols = slice(half * HALF, half * HALF + HALF)
                        group_lo(g_s[1][:, o, cols], g_s[0][:, o, cols], m, split_count(b, G_G + m))
                    for m in range(TT):
                        group_lo(u_t[1][:, m, :], u_t[0][:, m, :], m, split_count(b, G_U + m))
                    for st in range(STEPS1):
                        if not last and st == 2:
                            rough_rsqrt(b * 2 + 2)
                        if not last and st in NEXT_STEPS:
                            j = NEXT_STEPS[st]
                            qkv_lo(j, split_count(b, G_NEXT + j))
                        for q in range(QUARTERS):
                            for k in range(2):
                                if st == 2 * q + 3 + k:
                                    pool.wait_ge(pvs_full, b * PVS + (PV0 + 2 * q + k + 2))
                                    xs = x1[:, 2 * k:2 * k + 2, 256 * q:256 * q + 256]
                                    g.tensor_tensor(xs, pvs[:, k, :].rearrange("p (i t) -> p i t", i=2), xs, ALU.add)\
                                     .then_inc(pvs_used, 1)

                per_batch(pool, batch)


_VECTORS = ("L0_conv_norm_w", "L0_conv_norm_b", "L0_conv_qkv_b", "L0_conv_proj_b", "L1_conv_gn_gamma",
            "L1_conv_gn_beta", "L1_conv_q_b", "L1_conv_v_b", "L1_conv_proj_b")


def kernel(**inputs):
    import concourse.bacc as bacc
    from concourse.bass_utils import run_bass_kernel_spmd

    nc = bacc.Bacc("TRN2", target_bir_lowering=False, num_devices=1)
    norm_group = np.arange(P) // GROUP
    same = norm_group[:, None] == norm_group[None, :]


    def by_kind(a):
        a = np.asarray(a)
        return a.reshape(HEADS, 3, CH, -1).swapaxes(0, 1).reshape(a.shape)

    vectors = {n: np.asarray(inputs[n]) for n in _VECTORS}
    vectors["L0_conv_qkv_b"] = by_kind(inputs["L0_conv_qkv_b"])
    arrays = {
        "x": np.asarray(inputs["x"]).reshape(B, C, T),
        "consts": np.concatenate([np.eye(P), same / GROUP], axis=1).astype(np.float32),
        "w_vectors": np.concatenate([vectors[n].reshape(-1, P).T for n in _VECTORS], axis=1),
        "w_gain1": np.asarray(inputs["L1_conv_gn_gamma"]),
        "w_qkv_t": by_kind(inputs["L0_conv_qkv_w"]).T,
        "w_p0_t": np.asarray(inputs["L0_conv_proj_w"]).T,
        "w_q1": np.asarray(inputs["L1_conv_q_w"]),
        "w_k1": np.asarray(inputs["L1_conv_k_w"]),
        "w_v1": np.asarray(inputs["L1_conv_v_w"]),
        "w_p1_t": np.asarray(inputs["L1_conv_proj_w"]).T,
    }
    arrays = {k: np.ascontiguousarray(a) for k, a in arrays.items()}
    ap = {k: nc.dram_tensor(k, list(a.shape), F32, kind="ExternalInput").ap() for k, a in arrays.items()}
    y = nc.dram_tensor("y", [B, C, T], F32, kind="ExternalOutput").ap()
    scratch = nc.dram_tensor("w_pairs", [PAIRS, P, 2 * CT * 3 * P], F16).ap()
    scratch_b = nc.dram_tensor("b_pairs", [PAIRS, P, 2], F32).ap()
    build(nc, ap["x"], {k[2:]: v for k, v in ap.items() if k.startswith("w_")}, y, ap["consts"], scratch, scratch_b)
    r = run_bass_kernel_spmd(nc, [arrays], core_ids=[0])
    return np.asarray(r.results[0]["y"]).reshape(B, C, 32, 32)
```

```python
from contextlib import ExitStack

import numpy as np
import concourse.bass as bass
from concourse import mybir

F32 = mybir.dt.float32
F16 = mybir.dt.float16
ALU = mybir.AluOpType
ACT = mybir.ActivationFunctionType
AX = mybir.AxisListType
ABSMAX = bass.bass_isa.ReduceOp.max

P = 128
B, C, T = 8, 512, 1024
CT = C // P
TT = T // P
HALF = 512
HEADS = 8
CH = C // HEADS
PAIRS = HEADS // 2
GROUP = C // 32
EPS0, EPS1 = 1e-5, 1e-6

WSC = 512.0
ZSC = 64.0
QSC = 1.0 / (WSC * ZSC * 2)
PSC = 4096.0

UNITS_PAIR = 2 * TT
UNITS0 = PAIRS * UNITS_PAIR
UNITS = UNITS0 + TT
QUARTERS = TT // 2
PV_PAIR = QUARTERS
PV0 = PAIRS * PV_PAIR
PVS = PV0 + 2 * QUARTERS
FILL = 6
G_PROJ0 = (PAIRS - 1) * FILL
G_PROJ1 = G_PROJ0 + CT
G_G = G_PROJ1 + CT
G_U = G_G + 2 * CT
G_NEXT = G_U + TT
GROUPS = G_NEXT + FILL
SPLITS = GROUPS - 2 * CT
STACK_INC = 4 * 16
V_INC = W_INC = 2 * 16

LAG0 = 3
PV_LAG = UNITS_PAIR // QUARTERS + LAG0
STEPS0 = UNITS_PAIR + PV_LAG + 1
AHEAD = 7
SLOTS = 4


def spread_chunks(first_step, per_step):
    steps, n = {}, 0
    for st, k in enumerate(per_step, first_step):
        steps[st] = [divmod(n + i, 4) for i in range(k)]
        n += k
    return steps


FILL_CHUNKS = spread_chunks(AHEAD, (2,) * 8 + (2, 2, 1, 1, 1, 1))
PROJ_CHUNKS = spread_chunks(17, (2, 2, 2, 2, 2, 3, 3))
NEXT_CHUNKS = spread_chunks(4, (4,) * FILL)
NEXT_AHEAD = {9: (0, 1), 10: (2,), 11: (3, 4, 5, 6)}
STEPS1 = TT + 4


def finished(chunks, st):
    return [j for j, i in chunks.get(st, ()) if i == 3]


def group_count(b, m):
    return b * GROUPS + (FILL + m + 1)


def split_count(b, m):
    return b * SPLITS + (FILL + (m if m < G_PROJ0 else m - 2 * CT) + 1)


def unit_count(b, n):
    return b * UNITS + (n + 1)


def staged_pv(b, v):
    return b * PVS + (v + 2)


def used_pv(b, v):
    return b * PVS + (v + 3)


def pair_unit(u):
    return (u % 4) // 2, 2 * (u // 4) + u % 2


def build(nc, x, w, y, consts, scratch, scratch_b):
    ctx = ExitStack()
    with ctx:
        def sb(name, cols, dt=F32):
            return ctx.enter_context(nc.sbuf_tensor(name, [P, cols], dt))

        def sem(name):
            return ctx.enter_context(nc.semaphore(name))

        def f16(ap):
            return ap.bitcast(F16)

        xin = sb("xin", CT * T)
        r2 = sb("x1_att", 2 * CT * T)
        r1 = sb("probs_t", 8192)
        r3 = sb("stacks_probs", 8192)
        z0buf = sb("z0", CT * T)
        natbuf = sb("nat", 3072)
        globuf = sb("g_lo", 2048)
        stgbuf = sb("staging", 2 * HALF)
        pvsbuf = sb("pv_staging", 2 * HALF)
        zstbuf = sb("z_staging", 2 * T)
        wcurbuf = sb("wqkv_pair", 1538)
        wp0 = sb("wp0", 2 * CT * C, F16)
        wm1 = sb("wm1", 2 * CT * C, F16)
        wu1 = sb("wu1", 2 * CT * C, F16)
        cst = sb("ident_gavg", 2 * P)
        ident16 = sb("ident16", P, F16)
        vec = sb("vectors", 64)
        small = sb("small", 160)

        xin_v = xin[:, :].rearrange("p (c t) -> p c t", c=CT)
        x1 = r2[:, 0:CT * T].rearrange("p (c t) -> p c t", c=CT)
        att = f16(r2[:, CT * T:]).rearrange("p (s c t) -> p s c t", s=2, c=CT)
        z1 = att
        z0 = f16(z0buf[:, :]).rearrange("p (s c t) -> p s c t", s=2, c=CT)
        probs_t = f16(r1[:, :]).rearrange("p (k h s j t) -> p k h s j t", k=2, h=2, s=2, j=TT)
        u_t = [f16(r1[:, 4096 * s + 2048:4096 * s + 4096]).rearrange("p (j o) -> p j o", j=TT) for s in range(2)]
        stacks = f16(r3[:, 0:3072]).rearrange("p (s h t) -> p s h t", s=3, h=2)
        v_cur = f16(r3[:, 3072:4096]).rearrange("p (s j c) -> p s j c", s=2, j=TT)
        probs32 = [r3[:, 4096:5120], r3[:, 5120:6144], zstbuf[:, 0:T], zstbuf[:, T:2 * T]]
        probs_hi = [f16(r3[:, 6144:6656]), f16(r3[:, 6656:7168]), f16(globuf[:, 0:512]), f16(globuf[:, 512:1024])]
        probs_lo = [f16(r3[:, 7168:7680]), f16(r3[:, 7680:8192]), f16(globuf[:, 1024:1536]), f16(globuf[:, 1536:2048])]
        g_s = [f16(r3[:, 0:2048]).rearrange("p (c t) -> p c t", c=CT),
               f16(globuf[:, :]).rearrange("p (c t) -> p c t", c=CT)]
        qk_nat = f16(natbuf[:, 0:2048]).rearrange("p (n s t) -> p n s t", n=2, s=2)
        v_nat = f16(natbuf[:, 2048:3072]).rearrange("p (s j c) -> p s j c", s=2, j=TT)
        stg = stgbuf[:, :].rearrange("p (k t) -> p k t", k=2)
        pvs = pvsbuf[:, :].rearrange("p (k t) -> p k t", k=2)
        zst = zstbuf[:, :].rearrange("p (k t) -> p k t", k=CT)
        w_cur = f16(wcurbuf[:, 0:1536]).rearrange("p (s c n o) -> p s c n o", s=2, c=CT, n=3)
        b_cur = wcurbuf[:, 1536:1538]
        wp0_v = wp0[:, :].rearrange("p (s c o) -> p s c o", s=2, c=CT)
        wm1_v = wm1[:, :].rearrange("p (s c o) -> p s c o", s=2, c=CT)
        wu1_v = wu1[:, :].rearrange("p (s c o) -> p s c o", s=2, c=CT)
        ident = cst[:, 0:P]
        gavg = cst[:, P:2 * P]

        w0t = r2[:, 0:6144].rearrange("p (c o) -> p c o", c=CT)
        wp0t = r2[:, 6144:8192].rearrange("p (c o) -> p c o", c=CT)
        wq1, wk1, wv1 = (r3[:, 2048 * i:2048 * i + 2048].rearrange("p (j c) -> p j c", j=CT) for i in range(3))
        m_raw = z0buf[:, 0:2048].rearrange("p (c o) -> p c o", c=CT)
        u_raw = z0buf[:, 2048:4096].rearrange("p (c o) -> p c o", c=CT)
        wp1t = globuf[:, :].rearrange("p (c o) -> p c o", c=CT)
        gain_row = stgbuf[:, 0:C]
        w0s = [f16(r1[:, 3072 * s:3072 * s + 3072]).rearrange("p (c n j o) -> p c n j o", c=CT, n=3, j=PAIRS)
               for s in range(2)]

        wp0_scaled = r1[:, 6144:8192].rearrange("p (c o) -> p c o", c=CT)
        m_gained, u_gained = (wide[:, :].bitcast(F32).rearrange("p (c o) -> p c o", c=CT) for wide in (wm1, wu1))

        gain0, shift0 = vec[:, 0:4], vec[:, 4:8]
        bqkv, bp0_in = vec[:, 8:20], vec[:, 20:24]
        gain1, shift1 = vec[:, 24:28], vec[:, 28:32]
        bq1, bv1, bp1_in = vec[:, 32:36], vec[:, 36:40], vec[:, 40:44]
        b_qkv = small[:, 0:12]
        b_g = small[:, 12:16]
        b_out1 = small[:, 16:20]
        b_out0 = small[:, 20:24]
        tops = small[:, 24:28]
        inv = small[:, 28:32]
        exp_scale = small[:, 32:34]
        out_scale = small[:, 34:36]
        b_qk = small[:, 36:44].rearrange("p (n j) -> p n j", n=2)
        tmp = small[:, 52:76]
        neg_half = small[:, 76:80]
        neg_max = small[:, 80:82]
        exp_bias = small[:, 82:84]
        row_sum = small[:, 84:86]
        row_inv = small[:, 86:88]
        row_scaled = small[:, 88:90]
        gn_stats = sb("gn_stats", CT * 12)
        gn = small[:, 96:144].rearrange("p (k c) -> p k c", c=CT)
        gn_sub = sb("gn_sub", 4 * CT)
        gn_parts = gn_stats[:, :].rearrange("p (c s k) -> p c s k", c=CT, s=4)

        scores = ctx.enter_context(nc.psum_tensor("scores", [P, 2, 2, HALF], F32))
        trans = ctx.enter_context(nc.psum_tensor("transposed", [P, 2, T], F16))
        pv = ctx.enter_context(nc.psum_tensor("pv", [P, HALF], F32))
        proj = ctx.enter_context(nc.psum_tensor("proj", [P, HALF], F32))

        loaded_qk, loaded_vp, loadedv = sem("loaded_qk"), sem("loaded_vp"), sem("loadedv")
        loaded_w0, loaded_wp0 = sem("loaded_w0"), sem("loaded_wp0")
        bank_filled, bank_read = sem("bank_filled"), sem("bank_read")
        bias_sums0, bias_sums1, bias0_ready, bias_proj = (sem("bias_sums0"), sem("bias_sums1"), sem("bias0_ready"),
                                                          sem("bias_proj"))
        factor0_ready, factor1_ready = sem("factor0_ready"), sem("factor1_ready")
        w_scaled, hi_for_pool, lo_by_pool = sem("w_scaled"), sem("hi_for_pool"), sem("lo_by_pool")
        tops_in, tops_out = sem("tops_in"), sem("tops_out")
        setup_chain = sem("setup_chain")
        w0_split, w0_stored = sem("w0_split"), sem("w0_stored")
        x_loaded = sem("x_loaded")
        pvs_full, pvs_used = sem("pvs_full"), sem("pvs_used")

        with nc.Block() as block:
            @block.sync
            def _(sp):
                def load_weights(dst, name, done):
                    sp.dma_start(dst, w[name].rearrange("(j p) c -> p j c", p=P)).then_inc(done, 16)

                load_weights(wq1, "q1", loaded_qk)
                load_weights(wk1, "k1", loaded_qk)
                sp.dma_start(vec[:, 0:44], w["vectors"]).then_inc(loadedv, 16)
                sp.dma_start(cst[:, :], consts).then_inc(loadedv, 16)
                sp.dma_start(gain_row, w["gain1"].rearrange("(a n) -> a n", a=1).broadcast_to([P, C])).then_inc(loadedv, 16)
                load_weights(w0t, "qkv_t", loaded_w0)
                load_weights(wv1, "v1", loaded_vp)
                load_weights(wp1t, "p1_t", loaded_vp)
                load_weights(wp0t, "p0_t", loaded_wp0)
                sp.dma_start(xin_v, x[0].rearrange("(c p) t -> p c t", p=P)).then_inc(x_loaded, 16)
                sp.wait_ge(w0_split, CT)
                for s in range(2):
                    for p in range(PAIRS + 1):
                        sp.dma_start(scratch[p, :, s * 1536:s * 1536 + 1536].rearrange("p (c n o) -> p c n o", c=CT, n=3),
                                     w0s[s][:, :, :, p % PAIRS, :]).then_inc(w0_stored, 16)
                for p in range(PAIRS + 1):
                    sp.dma_start(scratch_b[p], b_qk[:, :, p % PAIRS], allow_slow_non_contiguous=True).then_inc(w0_stored, 16)
                sp.wait_ge(w0_stored, 3 * (PAIRS + 1) * 16)

            @block.gpsimd
            def _(pool):
                nc.gpsimd.memset(neg_half, -0.5).then_inc(pvs_used, 2)
                pool.wait_ge(tops_in, 1)
                nc.gpsimd.partition_all_reduce(tops[:, 0:2], tmp[:, 0:2], P, ABSMAX).then_inc(tops_out, 1)
                pool.wait_ge(hi_for_pool, 1)
                nc.gpsimd.tensor_tensor(wp0_v[:, 1], wp0_scaled, wp0_v[:, 0], ALU.subtract).then_inc(lo_by_pool, 1)
                pool.wait_ge(tops_in, 2)
                nc.gpsimd.partition_all_reduce(tops[:, 2:4], tmp[:, 2:4], P, ABSMAX).then_inc(tops_out, 1)
                pool.wait_ge(hi_for_pool, 2)
                nc.gpsimd.tensor_tensor(wu1_v[:, 1], u_raw, wu1_v[:, 0], ALU.subtract).then_inc(lo_by_pool, 1)

            @block.tensor
            def _(pe):
                banks = [scores[:, k // 2, k % 2, :] for k in range(4)]
                def product(a_nat, b_v, fills):
                    for c, fill in enumerate(fills):
                        if fill >= CT:
                            pe.wait_ge(bank_read, fill - CT + 1)
                        for k in range(CT):
                            last = nc.tensor.matmul(banks[fill % CT], a_nat[:, k, c * P:c * P + P], b_v[:, k, :],
                                                    start=(k == 0), stop=(k == CT - 1))
                        last.then_inc(bank_filled, 1)

                def vector_sums(col, pairs):
                    for o in range(CT):
                        for k, (a, v) in enumerate(pairs):
                            for c in range(CT):
                                last = nc.tensor.matmul(proj[:, col + o:col + o + 1], a[:, c, o * P:o * P + P],
                                                        v[:, c:c + 1], start=(k + c == 0),
                                                        stop=(k == len(pairs) - 1 and c == CT - 1))
                    return last

                pe.wait_ge(loaded_qk, 2 * 16)
                product(wq1, wk1, range(CT))
                pe.wait_ge(loadedv, 3 * 16)
                pe.wait_ge(loaded_w0, 16)
                for n in range(3):
                    last = vector_sums(CT * n, [(w0t[:, :, n * C:n * C + C], shift0)])
                last.then_inc(bias_sums0, 1)
                pe.wait_ge(loaded_vp, 2 * 16)
                product(wv1, wp1t, range(CT, 2 * CT))
                pe.wait_ge(bank_read, 2 * CT)
                vector_sums(12, [(m_raw, shift1), (wk1, bq1)])
                vector_sums(16, [(u_raw, shift1), (wp1t, bv1)]).then_inc(bias_sums1, 1)
                pe.wait_ge(loaded_wp0, 16)
                pe.wait_ge(bias0_ready, 1)
                for o in range(CT):
                    for c in range(CT):
                        last = nc.tensor.matmul(pv[:, o:o + 1], wp0t[:, c, o * P:o * P + P], b_qkv[:, 8 + c:9 + c],
                                                start=(c == 0), stop=(c == CT - 1))
                last.then_inc(bias_proj, 1)

            @block.scalar
            def _(act):
                banks = [scores[:, k // 2, k % 2, :] for k in range(4)]
                def keep_product(raw, fills):
                    for c, fill in enumerate(fills):
                        act.wait_ge(bank_filled, fill + 1)
                        nc.scalar.activation(raw[:, c, :], banks[fill % CT], ACT.Copy).then_inc(bank_read, 1)

                keep_product(m_raw, range(CT))
                act.wait_ge(loadedv, 3 * 16)
                nc.scalar.activation(ident16[:, :], ident, ACT.Copy).then_inc(pvs_full, 1)
                act.wait_ge(factor0_ready, 1)
                for c in range(CT):
                    nc.scalar.activation(w0t[:, c, :], w0t[:, c, :], ACT.Copy, scale=tmp[:, 12 + c:13 + c]).then_inc(w_scaled, 1)
                keep_product(u_raw, range(CT, 2 * CT))
                nc.scalar.activation(wp0_scaled, wp0t, ACT.Copy, scale=inv[:, 1:2]).then_inc(w_scaled, 1)
                act.wait_ge(factor1_ready, 1)
                nc.scalar.activation(u_raw, u_gained, ACT.Copy, scale=inv[:, 3:4]).then_inc(w_scaled, 1)
                nc.scalar.activation(m_raw, m_gained, ACT.Copy, scale=inv[:, 2:3]).then_inc(w_scaled, 1)

            @block.vector
            def _(dve):
                chain = 0

                def step(ins):
                    nonlocal chain
                    chain += 1
                    ins.then_inc(setup_chain, 1)
                    dve.wait_ge(setup_chain, chain)

                v = nc.vector
                def top(dst, src, axes):
                    step(v.tensor_reduce(dst, src, axes, ALU.max, apply_absolute_value=True))

                dve.wait_ge(loadedv, 3 * 16)
                dve.wait_ge(loaded_w0, 16)
                for c in range(CT):
                    top(tmp[:, 8 + c:9 + c], w0t[:, c, :], AX.X)
                step(v.tensor_tensor(tmp[:, 8:12], tmp[:, 8:12], gain0, ALU.mult))
                top(tmp[:, 0:1], tmp[:, 8:12], AX.X)
                dve.wait_ge(loaded_wp0, 16)
                top(tmp[:, 1:2], wp0t, AX.XY)
                dve.wait_ge(bias_sums0, 1)
                v.tensor_tensor(b_qkv, proj[:, 0:12], bqkv, ALU.add).then_inc(bias0_ready, 1)
                dve.wait_ge(bias0_ready, 1)
                top(tmp[:, 4:5], b_qkv, AX.X)
                v.tensor_tensor(tmp[:, 0:1], tmp[:, 0:1], tmp[:, 4:5], ALU.max).then_inc(tops_in, 1)
                dve.wait_ge(tops_out, 1)
                step(v.tensor_scalar(tops[:, 0:2], tops[:, 0:2], 1e-30, None, ALU.max))
                step(v.reciprocal(tmp[:, 4:6], tops[:, 0:2]))
                step(v.tensor_scalar(inv[:, 0:2], tmp[:, 4:6], WSC, None, ALU.mult))
                v.tensor_scalar(tmp[:, 12:16], gain0, inv[:, 0:1], None, ALU.mult).then_inc(factor0_ready, 1)
                step(v.tensor_scalar(tmp[:, 16:17], tmp[:, 4:5], 0.5, None, ALU.mult))
                step(v.tensor_scalar(small[:, 36:44], b_qkv[:, 0:8], tmp[:, 16:17], None, ALU.mult))
                step(v.tensor_tensor(tmp[:, 6:8], tops[:, 0:2], tops[:, 0:1].broadcast_to([P, 2]), ALU.mult))
                step(v.tensor_scalar(exp_scale[:, 0:1], tmp[:, 6:7], 4.0 / CH ** 0.5, None, ALU.mult))
                step(v.tensor_scalar(out_scale[:, 0:1], tmp[:, 7:8], 2.0 / WSC, None, ALU.mult))
                for c in range(CT):
                    hi, lo = (w0s[k][:, c].rearrange("p n j o -> p (n j o)") for k in range(2))
                    dve.wait_ge(w_scaled, c + 1)
                    step(v.tensor_copy(hi, w0t[:, c, :]))
                    v.tensor_tensor(lo, w0t[:, c, :], hi, ALU.subtract).then_inc(w0_split, 1)
                for c in range(CT):
                    dve.wait_ge(bank_read, c + 1)
                    step(v.scalar_tensor_tensor(m_gained[:, c, :], m_raw[:, c, :], gain1[:, c:c + 1], gain_row,
                                                ALU.mult, ALU.mult))
                top(tmp[:, 2:3], m_gained, AX.XY)
                for c in range(CT):
                    dve.wait_ge(bank_read, CT + c + 1)
                    step(v.tensor_scalar(u_gained[:, c, :], u_raw[:, c, :], gain1[:, c:c + 1], None, ALU.mult))
                top(tmp[:, 3:4], u_gained, AX.XY)
                dve.wait_ge(w_scaled, CT + 1)
                v.tensor_copy(wp0_v[:, 0], wp0_scaled).then_inc(hi_for_pool, 1)
                dve.wait_ge(bias_sums1, 1)
                step(v.tensor_tensor(b_g, proj[:, 12:16], gain1, ALU.mult))
                step(v.tensor_tensor(b_out1, proj[:, 16:20], bp1_in, ALU.add))
                top(tmp[:, 5:6], b_g, AX.X)
                v.tensor_tensor(tmp[:, 2:3], tmp[:, 2:3], tmp[:, 5:6], ALU.max).then_inc(tops_in, 1)
                dve.wait_ge(tops_out, 2)
                step(v.tensor_scalar(tops[:, 2:4], tops[:, 2:4], 1e-30, None, ALU.max))
                step(v.reciprocal(tmp[:, 4:6], tops[:, 2:4]))
                v.tensor_scalar(inv[:, 2:4], tmp[:, 4:6], WSC, None, ALU.mult).then_inc(factor1_ready, 1)
                step(v.tensor_scalar(tmp[:, 17:18], tmp[:, 4:5], 0.5, None, ALU.mult))
                step(v.tensor_scalar(b_g, b_g, tmp[:, 17:18], None, ALU.mult))
                step(v.tensor_scalar(exp_scale[:, 1:2], tops[:, 2:3], 2.0 / (ZSC * C ** 0.5), None, ALU.mult))
                step(v.tensor_scalar(out_scale[:, 1:2], tops[:, 3:4], 2.0 / PSC, None, ALU.mult))
                dve.wait_ge(w_scaled, CT + 2)
                v.tensor_copy(wu1_v[:, 0], u_raw).then_inc(hi_for_pool, 1)
                dve.wait_ge(w_scaled, CT + 3)
                step(v.tensor_copy(wm1_v[:, 0], m_raw))
                step(v.tensor_tensor(wm1_v[:, 1], m_raw, wm1_v[:, 0], ALU.subtract))
                dve.wait_ge(bias_proj, 1)
                v.tensor_tensor(b_out0, pv[:, 0:4], bp0_in, ALU.add)

        y_stored = sem("y_stored")
        w_loaded = sem("w_loaded")
        stack_a, stack_b, v_moved = sem("stack_a"), sem("stack_b"), sem("v_moved")
        scores_done, neg_max_done, bias_done = sem("scores_done"), sem("neg_max_done"), sem("bias_done")
        exp_done, sum_scaled, inv_done = sem("exp_done"), sem("sum_scaled"), sem("inv_done")
        rescaled, rescaled_odd = sem("rescaled"), sem("rescaled_odd")
        hi_done, lo_done = sem("hi_done"), sem("lo_done")
        trans_hi, trans_lo = sem("trans_hi"), sem("trans_lo")
        kept_hi, kept_lo = sem("kept_hi"), sem("kept_lo")
        pv_done, pvs_hi = sem("pv_done"), sem("pvs_hi")
        group_done, stg_full, stg_hi, stg_used = sem("group_done"), sem("stg_full"), sem("stg_hi"), sem("stg_used")
        gn_in, gn_out, gn_chain = sem("gn_in"), sem("gn_out"), sem("gn_chain")
        pow_in, pow_out, z_coef = sem("pow_in"), sem("pow_out"), sem("z_coef")
        z32_done, z_hi, z_done0, z_done1 = sem("z32_done"), sem("z_hi"), sem("z_done0"), sem("z_done1")
        GN_CHAIN = 10

        def per_batch(eng, body):
            with eng.Fori(0, B - 1) as b:
                body(b, False)
            body(B - 1, True)

        def per_pair(eng, b, body):
            with eng.Fori(0, PAIRS - 1) as p:
                body(p, False)
            body(PAIRS - 1, True)

        def probs_t_of(u, s):
            head, tile = pair_unit(u)
            return probs_t[:, (u // 4) % 2, head, s, :, (tile % 2) * P:(tile % 2) * P + P]

        def free_within(v0):
            def free(u):
                return v0 + u // 4 - 1 if u % 4 == 0 and u >= 8 else None
            return free

        def free_across(v0):
            return lambda u: v0 - 1 if u == 0 else None

        def free_next_batch(v0):
            return lambda u: v0 if u == 2 else v0 - 2 if u == 0 else None

        def free1(v0, u):
            return v0 + 2 * (u // 2 - 1) if u % 2 == 0 and u >= 4 else None

        def free_nothing(u):
            return None

        def back(u):
            return SLOTS

        def back_first(u):
            return SLOTS if u >= SLOTS else None

        def back_next_batch(u):
            return 2 if u < 2 else SLOTS

        with nc.Block() as block:
            @block.sync
            def _(sp):
                def stacks_of(head, done):
                    rows = slice(head * CH, head * CH + CH)
                    low, high = slice(0, CH), slice(CH, P)
                    for dst, src in ((stacks[low, 1:3, head], qk_nat[rows, 1, :, :]),
                                     (stacks[high, 1:3, head], qk_nat[rows, 1, :, :]),
                                     (stacks[low, 0, head], qk_nat[rows, 0, 0, :]),
                                     (stacks[high, 0, head], qk_nat[rows, 0, 1, :])):
                        sp.dma_start(dst, src).then_inc(done, 16)

                def move_v(*halves):
                    for s in halves:
                        sp.dma_start(v_cur[:, s], v_nat[:, s]).then_inc(v_moved, 16)

                def load_x(b):
                    sp.dma_start(xin_v, x[b].rearrange("(c p) t -> p c t", p=P)).then_inc(x_loaded, 16)

                def load_w(p):
                    sp.dma_start(f16(wcurbuf[:, 0:1536]), scratch[p]).then_inc(w_loaded, 16)
                    sp.dma_start(b_cur, scratch_b[p]).then_inc(w_loaded, 16)

                load_w(0)
                sp.wait_ge(stg_used, 4)
                stacks_of(0, stack_a)
                stacks_of(1, stack_b)
                sp.wait_ge(stg_used, FILL)
                move_v(0, 1)
                load_w(1)

                def batch(b, last):
                    def pair(p, last_pair):
                        bp = b * UNITS + p * UNITS_PAIR
                        if not last_pair:
                            sp.wait_ge(stg_used, b * GROUPS + p * FILL + (FILL + 4))
                            sp.wait_ge(scores_done, bp + UNITS_PAIR - 2)
                            stacks_of(0, stack_a)
                            sp.wait_ge(scores_done, bp + UNITS_PAIR)
                            stacks_of(1, stack_b)
                            sp.wait_ge(group_done, b * GROUPS + p * FILL + 2 * FILL)
                            load_w(p + 2)
                            sp.wait_ge(stg_used, b * GROUPS + p * FILL + 2 * FILL)
                            sp.wait_ge(pv_done, b * PVS + p * PV_PAIR + PV_PAIR)
                            move_v(0, 1)

                    per_pair(sp, b, pair)
                    if not last:
                        sp.wait_ge(stg_used, group_count(b, G_G - 1))
                        load_x(b + 1)
                    for q in range(QUARTERS):
                        if q == 2 and not last:
                            sp.wait_ge(stg_used, group_count(b, G_NEXT + 3))
                            sp.wait_ge(scores_done, unit_count(b, UNITS - 1))
                            stacks_of(0, stack_a)
                            stacks_of(1, stack_b)
                        sp.wait_ge(pvs_used, used_pv(b, PV0 + 2 * q + 1))
                        cols = slice(256 * q, 256 * q + 256)
                        sp.dma_start(y[b].rearrange("(c p) t -> p c t", p=P)[:, :, cols], x1[:, :, cols])\
                          .then_inc(y_stored, 16)
                    if not last:
                        sp.wait_ge(stg_used, group_count(b, G_NEXT + 5))
                        load_w(1)
                        move_v(0)
                    sp.wait_ge(y_stored, (b * QUARTERS + QUARTERS) * 16)
                    if not last:
                        move_v(1)

                per_batch(sp, batch)

            @block.tensor
            def _(pe):
                THREE = ((0, 0), (0, 1), (1, 0))

                def products(out, terms, first, last):
                    for i, (lhs, rhs) in enumerate(terms):
                        for k, (a, c) in enumerate(THREE):
                            mm = nc.tensor.matmul(out, lhs(a), rhs(c), start=(first and i + k == 0),
                                                  stop=(last and i == len(terms) - 1 and k == 2))
                    return mm

                def group(out, terms):
                    return products(out, terms, True, True)

                def qkv_chunk(j, i):
                    if j < 4:
                        n, cols = (1, 0)[j // 2], slice((j % 2) * HALF, (j % 2) * HALF + HALF)
                        return products(proj[:, :], [(lambda s: w_cur[:, s, i, n, :], lambda s: z0[:, s, i, cols])],
                                        i == 0, i == 3)
                    rows = slice((4 * (j - 4) + i) * P, (4 * (j - 4) + i) * P + P)
                    return group(proj[:, i * P:i * P + P],
                                 [(lambda s, c=c: z0[:, s, c, rows], lambda s, c=c: w_cur[:, s, c, 2, :])
                                  for c in range(CT)])

                def qkv_chunks(chunks, count):
                    for j, i in chunks:
                        if i == 0:
                            pe.wait_ge(stg_full, count + j)
                        mm = qkv_chunk(j, i)
                        if i == 3:
                            mm.then_inc(group_done, 1)

                def transpose(n, slot, s, first=False):
                    ready, done, kept = ((hi_done, trans_hi, kept_hi), (lo_done, trans_lo, kept_lo))[s]
                    src = (probs_hi, probs_lo)[s]
                    if not first:
                        pe.wait_ge(kept, n - 1)
                    pe.wait_ge(ready, n)
                    for j in range(TT):
                        last = nc.tensor.transpose(trans[:, s, j * P:j * P + P], src[slot][:, j * P:j * P + P],
                                                   ident16[:, :])
                    last.then_inc(done, 1)

                def scores0(n0, st, moved, prologue=False):
                    head, tile = pair_unit(st)
                    if st in (0, 2):
                        pe.wait_ge((stack_a, stack_b)[head], moved * STACK_INC)
                    if not (prologue and st < 2):
                        pe.wait_ge(exp_done, n0 + st - 1)
                    for half in range(2):
                        cols = slice(half * HALF, half * HALF + HALF)
                        for k in range(2):
                            mm = nc.tensor.matmul(scores[:, st % 2, half, :],
                                                  stacks[:, 0, head, tile * P:tile * P + P],
                                                  stacks[:, 1 + k, head, cols], start=(k == 0), stop=(k == 1))
                    mm.then_inc(scores_done, 1)

                def unit_step(n0, st, moved, prologue=False, between=lambda: None):
                    if st < UNITS_PAIR:
                        scores0(n0, st, moved, prologue)
                    u = st - LAG0
                    if 0 <= u < UNITS_PAIR:
                        transpose(n0 + (u + 1), u % SLOTS, 0, first=prologue and u == 0)
                    between()
                    if 0 <= u < UNITS_PAIR:
                        transpose(n0 + (u + 1), u % SLOTS, 1, first=prologue and u == 0)

                def gn_sums(n):
                    for k in range(2):
                        pe.wait_ge(gn_in, 2 * n + (k + 1))
                        nc.tensor.matmul(proj[:, k * CT:k * CT + CT], gavg,
                                         gn[:, 0, :] if k == 0 else gn[:, 3, :],
                                         start=True, stop=True).then_inc(gn_out, 1)

                gn_sums(0)
                pe.wait_ge(z_done0, CT)
                pe.wait_ge(w_loaded, W_INC)
                for j in range(FILL):
                    if j:
                        pe.wait_ge(stg_full, j)
                    if j == 1:
                        pe.wait_ge(z_done1, CT)
                    for i in range(4):
                        mm = qkv_chunk(j, i)
                    mm.then_inc(group_done, 1)
                for st in range(AHEAD):
                    unit_step(0, st, 1, prologue=True)

                def batch(b, last):
                    def pair(p, last_pair):
                        n0 = b * UNITS + p * UNITS_PAIR
                        v0 = b * PVS + p * PV_PAIR
                        m0 = b * GROUPS + p * FILL + FILL
                        moved = b * PAIRS + p + 1

                        def pv_chunk(st):
                            for q in range(QUARTERS):
                                j = st - (4 * q + PV_LAG)
                                if 0 <= j < 4:
                                    if j == 0:
                                        pe.wait_ge(kept_hi, n0 + 4 * q + 4)
                                        pe.wait_ge(kept_lo, n0 + 4 * q + 4)
                                        pe.wait_ge(pvs_full, v0 + q + 1)
                                        if q == 0:
                                            pe.wait_ge(v_moved, moved * V_INC)
                                    for kt in (2 * j, 2 * j + 1):
                                        for i, (a, c) in enumerate(THREE):
                                            for head in range(2):
                                                mm = nc.tensor.matmul(
                                                    pv[head * CH:head * CH + CH, 0:256],
                                                    v_cur[:, a, kt, head * CH:head * CH + CH],
                                                    probs_t[:, q % 2, head, c, kt, :],
                                                    start=(kt == 0 and i == 0), stop=(kt == TT - 1 and i == 2))
                                    if j == 3:
                                        mm.then_inc(pv_done, 1)

                        def fill(st):
                            pv_chunk(st)
                            if not last_pair:
                                if st == AHEAD:
                                    pe.wait_ge(w_loaded, (b * PAIRS + p + 2) * W_INC)
                                qkv_chunks(FILL_CHUNKS.get(st, ()), m0)
                                return
                            for o, i in PROJ_CHUNKS.get(st, ()):
                                if o + i == 0:
                                    pe.wait_ge(pvs_used, used_pv(b, p * PV_PAIR + 1))
                                if i == 0:
                                    pe.wait_ge(stg_full, group_count(b, G_PROJ0 + o - 1))
                                mm = out_proj_chunk(o, 0, proj, i)
                                if i == 3:
                                    mm.then_inc(group_done, 1)

                        for st in range(AHEAD, STEPS0):
                            ahead = st - (STEPS0 - AHEAD)
                            if last_pair or ahead < 0:
                                unit_step(n0, st, moved, between=lambda: fill(st))
                            else:
                                unit_step(n0, st, moved)
                                unit_step(n0 + UNITS_PAIR, ahead, moved + 1, between=lambda: fill(st))

                    def out_proj_chunk(o, half, bank, i):
                        cols = slice(half * HALF, half * HALF + HALF)
                        return products(bank[:, :], [(lambda s: wp0_v[:, s, i, o * P:o * P + P],
                                                      lambda s: att[:, s, i, cols])], i == 0, i == 3)

                    per_pair(pe, b, pair)

                    banks = (proj, pv)
                    for o in range(CT):
                        if o == 0:
                            pe.wait_ge(pvs_used, used_pv(b, PV0 - 1))
                        pe.wait_ge(stg_full, group_count(b, G_PROJ1 + o - (1 if o == 0 else 2)))
                        for i in range(4):
                            mm = out_proj_chunk(o, 1, banks[o % 2], i)
                        mm.then_inc(group_done, 1)
                    pe.wait_ge(stg_full, group_count(b, G_G - 1))
                    gn_sums(b * 2 + 1)
                    for m in range(2 * CT):
                        half, o = m // CT, m % CT
                        cols = slice(half * HALF, half * HALF + HALF)
                        pe.wait_ge(stg_full, group_count(b, G_G + m - 2))
                        for c in range(CT):
                            if o == 0:
                                pe.wait_ge((z_done0, z_done1)[half], (b * 2 + 1) * CT + (c + 1))
                            mm = products(banks[m % 2][:, :], [(lambda s: wm1_v[:, s, c, o * P:o * P + P],
                                                                lambda s: z1[:, s, c, cols])], c == 0, c == CT - 1)
                        mm.then_inc(group_done, 1)
                    for m in range(TT):
                        pe.wait_ge(stg_full, group_count(b, G_U + m - 2))
                        group(banks[m % 2][:, :], [(lambda s, c=c: z1[:, s, c, m * P:m * P + P],
                                                    lambda s, c=c: wu1_v[:, s, c, :]) for c in range(CT)])\
                            .then_inc(group_done, 1)

                    n0 = b * UNITS + UNITS0
                    v0 = b * PVS + PV0
                    for st in range(STEPS1):
                        if st < TT:
                            if st == 0:
                                pe.wait_ge(stg_used, group_count(b, G_U - 1))
                            pe.wait_ge(exp_done, n0 + st - 1)
                            for half in range(2):
                                cols = slice(half * HALF, half * HALF + HALF)
                                mm = group(scores[:, st % 2, half, :],
                                           [(lambda s, c=c: g_s[s][:, c, st * P:st * P + P],
                                             lambda s, c=c: z1[:, s, c, cols]) for c in range(CT)])
                            mm.then_inc(scores_done, 1)
                        if not last and st == 3:
                            pe.wait_ge(stg_full, group_count(b, G_NEXT - 1))
                            gn_sums(b * 2 + 2)
                        if not last and st in NEXT_CHUNKS:
                            if st == 4:
                                pe.wait_ge(z_done0, (b * 2 + 3) * CT)
                                pe.wait_ge(z_done1, (b * 2 + 3) * CT)
                                pe.wait_ge(w_loaded, (b * PAIRS + PAIRS + 1) * W_INC)
                            qkv_chunks(NEXT_CHUNKS[st], group_count(b, G_NEXT - 1))
                        if not last and st in NEXT_AHEAD and st < 11:
                            for nst in NEXT_AHEAD[st]:
                                unit_step(b * UNITS + UNITS, nst, b * PAIRS + (PAIRS + 1))
                        for q in range(QUARTERS):
                            for k in range(2):
                                if st == 2 * q + 3 + k:
                                    if k == 0:
                                        pe.wait_ge(kept_hi, n0 + 2 * q + 2)
                                        pe.wait_ge(kept_lo, n0 + 2 * q + 2)
                                    if q == 0 and k == 0:
                                        pe.wait_ge(stg_used, group_count(b, G_NEXT - 1))
                                    pe.wait_ge(pvs_full, v0 + 2 * q + k + 1)
                                    for i in range(2):
                                        o = 2 * k + i
                                        mm = group(pv[:, 256 * i:256 * i + 256],
                                                   [(lambda s, kt=kt: u_t[s][:, kt, o * P:o * P + P],
                                                     lambda s, kt=kt: probs_t[:, q % 2, 0, s, kt, :])
                                                    for kt in range(TT)])
                                    mm.then_inc(pv_done, 1)
                        if not last and st == 11:
                            for nst in NEXT_AHEAD[st]:
                                unit_step(b * UNITS + UNITS, nst, b * PAIRS + (PAIRS + 1))
                        u = st - 1
                        if 0 <= u < TT:
                            transpose(n0 + (u + 1), u % 2, 0)
                            transpose(n0 + (u + 1), u % 2, 1)

                per_batch(pe, batch)

            @block.scalar
            def _(act):
                def exponentials(n, par, slot, layer, back):
                    act.wait_ge(bias_done, n)
                    if back is not None:
                        act.wait_ge(lo_done, n - back)
                    nc.scalar.activation(probs32[slot], scores[:, par, :, :].rearrange("p a t -> p (a t)"), ACT.Exp,
                                         bias=exp_bias[:, par:par + 1], scale=exp_scale[:, layer:layer + 1],
                                         accum_out=row_sum[:, par:par + 1]).then_inc(exp_done, 1)

                def rescale(n, par, slot):
                    act.wait_ge(inv_done, n)
                    nc.scalar.activation(probs32[slot], probs32[slot], ACT.Copy, scale=row_inv[:, par:par + 1])\
                      .then_inc(rescaled, 1)

                def keep_lo(n, dst, free):
                    act.wait_ge(trans_lo, n)
                    if free is not None:
                        act.wait_ge(pv_done, free)
                    nc.scalar.activation(dst, trans[:, 1, :].rearrange("p (j t) -> p j t", j=TT), ACT.Copy)\
                      .then_inc(kept_lo, 1)

                def unit_step(n0, st, free, back, between=lambda: None):
                    u = st - 1
                    if 0 <= u < UNITS_PAIR and u % 2 == 0:
                        rescale(n0 + (u + 1), 0, u % SLOTS)
                    if st < UNITS_PAIR:
                        exponentials(n0 + (st + 1), st % 2, st % SLOTS, 0, back(st))
                    between()
                    u = st - LAG0
                    if 0 <= u < UNITS_PAIR:
                        keep_lo(n0 + (u + 1), probs_t_of(u, 1), free(u))

                def stage(count, m, src, scale, bias, two_back=True):
                    act.wait_ge(group_done, count)
                    if two_back:
                        act.wait_ge(stg_used, count - 2)
                    if bias is None:
                        nc.scalar.activation(stg[:, m % 2, :], src, ACT.Copy, scale=scale).then_inc(stg_full, 1)
                    else:
                        nc.scalar.activation(stg[:, m % 2, :], src, ACT.Identity, scale=scale, bias=bias)\
                          .then_inc(stg_full, 1)

                def qkv_stage(count, j, two_back=True):
                    n = (1, 0)[j // 2] if j < 4 else None
                    bias = None if n is None else b_cur[:, n:n + 1]
                    stage(count, j, proj[:, :], QSC, bias, two_back)

                def normalise(src, count, first=False):
                    act.wait_ge(z_coef, count)
                    for half in range(2):
                        for c in range(CT):
                            if half == 1:
                                act.wait_ge(z_done0, (count - 1) * CT + (c + 1))
                            elif not first:
                                act.wait_ge(z_done1, (count - 2) * CT + (c + 1))
                            nc.scalar.activation(zst[:, c, :], src[:, c, half * HALF:half * HALF + HALF], ACT.Identity,
                                                 scale=gn[:, 8, c:c + 1], bias=gn[:, 9, c:c + 1]).then_inc(z32_done, 1)

                act.wait_ge(x_loaded, 16)
                normalise(xin_v, 1, first=True)
                for j in range(FILL):
                    qkv_stage(j + 1, j, two_back=j >= 2)
                for st in range(AHEAD):
                    unit_step(0, st, free_nothing, back_first)

                def batch(b, last):
                    def pair(p, last_pair):
                        n0 = b * UNITS + p * UNITS_PAIR
                        v0 = b * PVS + p * PV_PAIR
                        m0 = b * GROUPS + p * FILL + FILL
                        def others(st):
                            for q in range(QUARTERS):
                                if st == 4 * q + PV_LAG + 3:
                                    act.wait_ge(pv_done, v0 + (q + 1))
                                    act.wait_ge(pvs_used, v0 + (q + 1))
                                    nc.scalar.activation(pvs[:, q % 2, 0:256], pv[:, 0:256], ACT.Copy, scale=1.0 / PSC)\
                                      .then_inc(pvs_full, 1)
                            if not last_pair:
                                for j in finished(FILL_CHUNKS, st):
                                    qkv_stage(m0 + (j + 1), j)
                            else:
                                for o in finished(PROJ_CHUNKS, st):
                                    stage(group_count(b, G_PROJ0 + o), o, proj[:, :], out_scale[:, 0:1],
                                          b_out0[:, o:o + 1])

                        for st in range(AHEAD, STEPS0):
                            ahead = st - (STEPS0 - AHEAD)
                            if last_pair or ahead < 0:
                                unit_step(n0, st, free_within(v0), back, between=lambda: others(st))
                            else:
                                unit_step(n0, st, free_within(v0), back)
                                unit_step(n0 + UNITS_PAIR, ahead, free_across(v0 + PV_PAIR), back,
                                          between=lambda: others(st))

                    per_pair(act, b, pair)
                    banks = (proj, pv)
                    for o in range(CT):
                        stage(group_count(b, G_PROJ1 + o), o, banks[o % 2][:, :], out_scale[:, 0:1], b_out0[:, o:o + 1])
                    normalise(x1, b * 2 + 2)
                    for m in range(2 * CT):
                        stage(group_count(b, G_G + m), m, banks[m % 2][:, :], QSC, b_g[:, m % CT:m % CT + 1])
                    for m in range(TT):
                        stage(group_count(b, G_U + m), m, banks[m % 2][:, :], QSC, None)
                    n0 = b * UNITS + UNITS0
                    v0 = b * PVS + PV0
                    for st in range(STEPS1):
                        if 0 <= st - 1 < TT and (st - 1) % 2 == 0:
                            rescale(n0 + st, 0, 0)
                        if st < TT:
                            exponentials(n0 + (st + 1), st % 2, st % 2, 1, 2)
                        if not last and st == 3:
                            normalise(xin_v, b * 2 + 3)
                        if not last:
                            for j in finished(NEXT_CHUNKS, st):
                                qkv_stage(group_count(b, G_NEXT + j), j)
                            if st in NEXT_AHEAD and st < 11:
                                for nst in NEXT_AHEAD[st]:
                                    unit_step(b * UNITS + UNITS, nst, free_next_batch(b * PVS + PVS), back_next_batch)
                        for q in range(QUARTERS):
                            for k in range(2):
                                if st == 2 * q + 3 + k:
                                    act.wait_ge(pv_done, v0 + (2 * q + k + 1))
                                    act.wait_ge(pvs_used, v0 + (2 * q + k + 1))
                                    for i in range(2):
                                        o = 2 * k + i
                                        cp = nc.scalar.activation(pvs[:, k, 256 * i:256 * i + 256],
                                                                  pv[:, 256 * i:256 * i + 256], ACT.Identity,
                                                                  scale=out_scale[:, 1:2], bias=b_out1[:, o:o + 1])
                                    cp.then_inc(pvs_full, 1)
                        if not last and st == 11:
                            for nst in NEXT_AHEAD[st]:
                                unit_step(b * UNITS + UNITS, nst, free_next_batch(b * PVS + PVS), back_next_batch)
                        u = st - 1
                        if 0 <= u < TT:
                            keep_lo(n0 + (u + 1), probs_t[:, (u // 2) % 2, 0, 1, :, (u % 2) * P:(u % 2) * P + P],
                                    free1(v0, u))

                per_batch(act, batch)

            @block.vector
            def _(dve):
                v = nc.vector

                def row_max(n, par, layer):
                    dve.wait_ge(scores_done, n)
                    v.tensor_reduce(neg_max[:, par:par + 1], scores[:, par, :, :], AX.XY, ALU.max, negate=True)\
                     .then_inc(neg_max_done, 1)
                    dve.wait_ge(neg_max_done, n)
                    v.tensor_scalar(exp_bias[:, par:par + 1], neg_max[:, par:par + 1], exp_scale[:, layer:layer + 1],
                                    None, ALU.mult).then_inc(bias_done, 1)

                def row_inverse(n, par):
                    dve.wait_ge(exp_done, n)
                    v.tensor_scalar(row_scaled[:, par:par + 1], row_sum[:, par:par + 1], 1.0 / PSC, None, ALU.mult)\
                     .then_inc(sum_scaled, 1)
                    dve.wait_ge(sum_scaled, n)
                    v.reciprocal(row_inv[:, par:par + 1], row_scaled[:, par:par + 1]).then_inc(inv_done, 1)

                def split(n, h, par, slot, back):
                    if par == 1:
                        dve.wait_ge(inv_done, n)
                        v.tensor_scalar(probs32[slot], probs32[slot], row_inv[:, par:par + 1], None, ALU.mult)\
                         .then_inc(rescaled_odd, 1)
                        dve.wait_ge(rescaled_odd, h)
                    else:
                        dve.wait_ge(rescaled, h)
                    if back is not None:
                        dve.wait_ge(trans_hi, n - back)
                    v.tensor_copy(probs_hi[slot], probs32[slot]).then_inc(hi_done, 1)

                def keep_hi(n, dst, free):
                    dve.wait_ge(trans_hi, n)
                    if free is not None:
                        dve.wait_ge(pv_done, free)
                    v.tensor_copy(dst, trans[:, 0, :].rearrange("p (j t) -> p j t", j=TT)).then_inc(kept_hi, 1)

                def unit_step(n0, h0, st, free, back):
                    if 0 <= st - 1 < UNITS_PAIR:
                        row_inverse(n0 + st, (st - 1) % 2)
                    if st < UNITS_PAIR:
                        row_max(n0 + (st + 1), st % 2, 0)
                    if 0 <= st - 1 < UNITS_PAIR:
                        split(n0 + st, h0 + ((st - 1) // 2 + 1), (st - 1) % 2, (st - 1) % SLOTS, back(st - 1))
                    u = st - LAG0
                    if 0 <= u < UNITS_PAIR:
                        keep_hi(n0 + (u + 1), probs_t_of(u, 0), free(u))

                def group_hi(dst, m, count):
                    dve.wait_ge(stg_full, count)
                    v.tensor_copy(dst, stg[:, m % 2, :]).then_inc(stg_hi, 1)

                def qkv_hi(j, count):
                    if j < 4:
                        cols = slice((j % 2) * HALF, (j % 2) * HALF + HALF)
                        group_hi(qk_nat[:, (1, 0)[j // 2], 0, cols], j, count)
                    else:
                        group_hi(v_nat[:, 0, 4 * (j - 4):4 * (j - 4) + 4, :].rearrange("p j c -> p (j c)"), j, count)

                def stats(src, c, half):
                    v.bn_stats(gn_stats[:, c * 12 + half * 6:c * 12 + half * 6 + 6],
                               src[:, c, half * HALF:half * HALF + HALF]).then_inc(gn_chain, 1)

                def norm_coefficients(k, eps):
                    base = k * (8 + GN_CHAIN)
                    done = [8]

                    def step(ins):
                        done[0] += 1
                        ins.then_inc(gn_chain, 1)
                        dve.wait_ge(gn_chain, base + done[0])

                    part_mean, part_sq = gn_parts[:, :, :, 1], gn_parts[:, :, :, 2]
                    d = gn_sub[:, :].rearrange("p (c s) -> p c s", c=CT)
                    g_mean, spread, e, r, t = (gn[:, i, :] for i in (2, 3, 4, 5, 6))
                    dve.wait_ge(gn_chain, base + 8)
                    v.tensor_reduce(gn[:, 0, :], part_mean, AX.X, ALU.add).then_inc(gn_in, 1)
                    dve.wait_ge(gn_out, 2 * k + 1)
                    step(v.tensor_scalar(g_mean, proj[:, 0:CT], 0.25, None, ALU.mult))
                    for c in range(CT):
                        ins = v.tensor_scalar(d[:, c, :], part_mean[:, c, :], g_mean[:, c:c + 1], None, ALU.subtract)
                    step(ins)
                    step(v.tensor_tensor(d, d, d, ALU.mult))
                    step(v.scalar_tensor_tensor(d, d, T / 4.0, part_sq, ALU.mult, ALU.add))
                    v.tensor_reduce(spread, d, AX.X, ALU.add).then_inc(gn_in, 1)
                    dve.wait_ge(gn_out, 2 * k + 2)
                    v.tensor_scalar(e, proj[:, CT:2 * CT], 1.0 / T, eps, ALU.mult, ALU.add).then_inc(pow_in, 1)
                    dve.wait_ge(pow_out, k + 1)
                    step(v.tensor_tensor(t, r, r, ALU.mult))
                    step(v.tensor_tensor(t, t, e, ALU.mult))
                    step(v.tensor_scalar(t, t, -0.5, 1.5, ALU.mult, ALU.add))
                    step(v.tensor_tensor(t, t, r, ALU.mult))
                    step(v.tensor_scalar(gn[:, 8, :], t, ZSC, None, ALU.mult))
                    step(v.tensor_tensor(t, g_mean, gn[:, 8, :], ALU.mult))
                    v.tensor_scalar(gn[:, 9, :], t, -1.0, None, ALU.mult).then_inc(z_coef, 1)
                    assert done[0] == 8 + GN_CHAIN

                def norm_split(dst, k):
                    for half in range(2):
                        cols = slice(half * HALF, half * HALF + HALF)
                        for c in range(CT):
                            n = k * 2 * CT + (half * CT + c + 1)
                            dve.wait_ge(z32_done, n)
                            v.tensor_copy(dst[:, 0, c, cols], zst[:, c, :]).then_inc(z_hi, 1)
                            if half == 0:
                                dve.wait_ge(z_hi, n)
                                v.tensor_tensor(dst[:, 1, c, cols], zst[:, c, :], dst[:, 0, c, cols], ALU.subtract)\
                                 .then_inc(z_done0, 1)

                def all_stats(src):
                    for c in range(CT):
                        for half in range(2):
                            stats(src, c, half)

                dve.wait_ge(x_loaded, 16)
                all_stats(xin_v)
                norm_coefficients(0, EPS0)
                norm_split(z0, 0)
                for j in range(FILL):
                    qkv_hi(j, j + 1)
                for st in range(AHEAD):
                    unit_step(0, 0, st, free_nothing, back_first)

                def batch(b, last):
                    def pair(p, last_pair):
                        n0 = b * UNITS + p * UNITS_PAIR
                        v0 = b * PVS + p * PV_PAIR
                        m0 = b * GROUPS + p * FILL + FILL
                        h0 = b * (UNITS // 2) + p * (UNITS_PAIR // 2)
                        for st in range(AHEAD, STEPS0):
                            unit_step(n0, h0, st, free_within(v0), back)
                            ahead = st - (STEPS0 - AHEAD)
                            if not last_pair and ahead >= 0:
                                unit_step(n0 + UNITS_PAIR, h0 + UNITS_PAIR // 2, ahead, free_across(v0 + PV_PAIR), back)
                            if not last_pair:
                                for j in finished(FILL_CHUNKS, st):
                                    qkv_hi(j, m0 + (j + 1))
                            for q in range(QUARTERS):
                                if st == 4 * q + PV_LAG + 4:
                                    dve.wait_ge(pvs_full, v0 + (q + 2))
                                    v.tensor_copy(att[:, 0, bass.ds(p, 1), 256 * q:256 * q + 256].rearrange("p a t -> p (a t)")
                                                  if not isinstance(p, int) else att[:, 0, p, 256 * q:256 * q + 256],
                                                  pvs[:, q % 2, 0:256]).then_inc(pvs_hi, 1)

                    per_pair(dve, b, pair)
                    for half in range(2):
                        for c in range(CT):
                            dve.wait_ge(stg_used, group_count(b, (G_PROJ0, G_PROJ1)[half] + c))
                            stats(x1, c, half)
                    norm_coefficients(b * 2 + 1, EPS1)
                    norm_split(z1, b * 2 + 1)
                    for m in range(2 * CT):
                        half, o = m // CT, m % CT
                        group_hi(g_s[0][:, o, half * HALF:half * HALF + HALF], m, group_count(b, G_G + m))
                    for m in range(TT):
                        group_hi(u_t[0][:, m, :], m, group_count(b, G_U + m))
                    n0 = b * UNITS + UNITS0
                    h0 = b * (UNITS // 2) + UNITS0 // 2
                    v0 = b * PVS + PV0
                    for st in range(STEPS1):
                        u = st - 1
                        if 0 <= u < TT:
                            row_inverse(n0 + (u + 1), u % 2)
                            split(n0 + (u + 1), h0 + (u // 2 + 1), u % 2, u % 2, 2)
                        if st < TT:
                            row_max(n0 + (st + 1), st % 2, 1)
                        if not last:
                            for j in finished(NEXT_CHUNKS, st):
                                qkv_hi(j, group_count(b, G_NEXT + j))
                            if st in NEXT_AHEAD:
                                for nst in NEXT_AHEAD[st]:
                                    unit_step(b * UNITS + UNITS, b * (UNITS // 2) + UNITS // 2, nst,
                                              free_next_batch(b * PVS + PVS), back_next_batch)
                        if 0 <= u < TT:
                            keep_hi(n0 + (u + 1), probs_t[:, (u // 2) % 2, 0, 0, :, (u % 2) * P:(u % 2) * P + P],
                                    free1(v0, u))
                        if not last and st == 2:
                            dve.wait_ge(x_loaded, (b + 2) * 16)
                            all_stats(xin_v)
                            norm_coefficients(b * 2 + 2, EPS0)
                        if not last and st == 3:
                            norm_split(z0, b * 2 + 2)

                per_batch(dve, batch)

            @block.gpsimd
            def _(pool):
                g = nc.gpsimd

                def group_lo(lo, hi, m, count):
                    pool.wait_ge(stg_hi, count)
                    g.tensor_tensor(lo, stg[:, m % 2, :], hi, ALU.subtract).then_inc(stg_used, 1)

                def qkv_lo(j, count):
                    if j < 4:
                        n, cols = (1, 0)[j // 2], slice((j % 2) * HALF, (j % 2) * HALF + HALF)
                        group_lo(qk_nat[:, n, 1, cols], qk_nat[:, n, 0, cols], j, count)
                    else:
                        rows = slice(4 * (j - 4), 4 * (j - 4) + 4)
                        group_lo(v_nat[:, 1, rows, :].rearrange("p j c -> p (j c)"),
                                 v_nat[:, 0, rows, :].rearrange("p j c -> p (j c)"), j, count)

                def residual0(b, m, c, half):
                    pool.wait_ge(stg_full, group_count(b, m))
                    cols = slice(half * HALF, half * HALF + HALF)
                    g.tensor_tensor(x1[:, c, cols], stg[:, m % 2, :], xin_v[:, c, cols], ALU.add).then_inc(stg_used, 1)

                def rough_rsqrt(k):
                    pool.wait_ge(pow_in, k + 1)
                    g.tensor_tensor(gn[:, 5, :], gn[:, 4, :], neg_half, ALU.pow).then_inc(pow_out, 1)

                def split_lo(n, slot, back):
                    pool.wait_ge(hi_done, n)
                    if back is not None:
                        pool.wait_ge(trans_lo, n - back)
                    g.tensor_tensor(probs_lo[slot], probs32[slot], probs_hi[slot], ALU.subtract).then_inc(lo_done, 1)

                def unit_step(n0, st, back):
                    if 0 <= st - 1 < UNITS_PAIR:
                        split_lo(n0 + st, (st - 1) % SLOTS, back(st - 1))

                def norm_lo(dst, k):
                    for c in range(CT):
                        pool.wait_ge(z_hi, k * 2 * CT + (CT + c + 1))
                        g.tensor_tensor(dst[:, 1, c, HALF:T], zst[:, c, :], dst[:, 0, c, HALF:T], ALU.subtract)\
                         .then_inc(z_done1, 1)

                rough_rsqrt(0)
                norm_lo(z0, 0)
                for j in range(FILL):
                    qkv_lo(j, j + 1)
                for st in range(AHEAD):
                    unit_step(0, st, back_first)

                def batch(b, last):
                    def pair(p, last_pair):
                        v0 = b * PVS + p * PV_PAIR
                        s0 = b * SPLITS + p * FILL + FILL
                        n0 = b * UNITS + p * UNITS_PAIR
                        for st in range(AHEAD, STEPS0):
                            unit_step(n0, st, back)
                            ahead = st - (STEPS0 - AHEAD)
                            if not last_pair and ahead >= 0:
                                unit_step(n0 + UNITS_PAIR, ahead, back)
                            if not last_pair:
                                for j in finished(FILL_CHUNKS, st):
                                    qkv_lo(j, s0 + (j + 1))
                            else:
                                for o in finished(PROJ_CHUNKS, st):
                                    residual0(b, G_PROJ0 + o, o, 0)
                            for q in range(QUARTERS):
                                if st == 4 * q + PV_LAG + 4:
                                    cols = slice(256 * q, 256 * q + 256)
                                    at = [att[:, s, bass.ds(p, 1), cols].rearrange("p a t -> p (a t)")
                                          if not isinstance(p, int) else att[:, s, p, cols] for s in range(2)]
                                    pool.wait_ge(pvs_hi, b * PV0 + p * PV_PAIR + (q + 1))
                                    g.tensor_tensor(at[1], pvs[:, q % 2, 0:256], at[0], ALU.subtract)\
                                     .then_inc(pvs_used, 1)

                    per_pair(pool, b, pair)
                    for o in range(CT):
                        residual0(b, G_PROJ1 + o, o, 1)
                    rough_rsqrt(b * 2 + 1)
                    norm_lo(z1, b * 2 + 1)
                    for m in range(2 * CT):
                        half, o = m // CT, m % CT
                        cols = slice(half * HALF, half * HALF + HALF)
                        group_lo(g_s[1][:, o, cols], g_s[0][:, o, cols], m, split_count(b, G_G + m))
                    for m in range(TT):
                        group_lo(u_t[1][:, m, :], u_t[0][:, m, :], m, split_count(b, G_U + m))
                    for st in range(STEPS1):
                        if 0 <= st - 1 < TT:
                            split_lo(b * UNITS + (UNITS0 + st), (st - 1) % 2, 2)
                        if not last and st == 2:
                            rough_rsqrt(b * 2 + 2)
                        if not last and st == 3:
                            norm_lo(z0, b * 2 + 2)
                        if not last:
                            for j in finished(NEXT_CHUNKS, st):
                                qkv_lo(j, split_count(b, G_NEXT + j))
                            for nst in NEXT_AHEAD.get(st, ()):
                                unit_step(b * UNITS + UNITS, nst, back_next_batch)
                        for q in range(QUARTERS):
                            for k in range(2):
                                if st == 2 * q + 3 + k:
                                    pool.wait_ge(pvs_full, b * PVS + (PV0 + 2 * q + k + 2))
                                    xs = x1[:, 2 * k:2 * k + 2, 256 * q:256 * q + 256]
                                    g.tensor_tensor(xs, pvs[:, k, :].rearrange("p (i t) -> p i t", i=2), xs, ALU.add)\
                                     .then_inc(pvs_used, 1)

                per_batch(pool, batch)


_VECTORS = ("L0_conv_norm_w", "L0_conv_norm_b", "L0_conv_qkv_b", "L0_conv_proj_b", "L1_conv_gn_gamma",
            "L1_conv_gn_beta", "L1_conv_q_b", "L1_conv_v_b", "L1_conv_proj_b")


def kernel(**inputs):
    import concourse.bacc as bacc
    from concourse.bass_utils import run_bass_kernel_spmd

    nc = bacc.Bacc("TRN2", target_bir_lowering=False, num_devices=1)
    norm_group = np.arange(P) // GROUP
    same = norm_group[:, None] == norm_group[None, :]


    def by_kind(a):
        a = np.asarray(a)
        return a.reshape(HEADS, 3, CH, -1).swapaxes(0, 1).reshape(a.shape)

    vectors = {n: np.asarray(inputs[n]) for n in _VECTORS}
    vectors["L0_conv_qkv_b"] = by_kind(inputs["L0_conv_qkv_b"])
    arrays = {
        "x": np.asarray(inputs["x"]).reshape(B, C, T),
        "consts": np.concatenate([np.eye(P), same / GROUP], axis=1).astype(np.float32),
        "w_vectors": np.concatenate([vectors[n].reshape(-1, P).T for n in _VECTORS], axis=1),
        "w_gain1": np.asarray(inputs["L1_conv_gn_gamma"]),
        "w_qkv_t": by_kind(inputs["L0_conv_qkv_w"]).T,
        "w_p0_t": np.asarray(inputs["L0_conv_proj_w"]).T,
        "w_q1": np.asarray(inputs["L1_conv_q_w"]),
        "w_k1": np.asarray(inputs["L1_conv_k_w"]),
        "w_v1": np.asarray(inputs["L1_conv_v_w"]),
        "w_p1_t": np.asarray(inputs["L1_conv_proj_w"]).T,
    }
    arrays = {k: np.ascontiguousarray(a) for k, a in arrays.items()}
    ap = {k: nc.dram_tensor(k, list(a.shape), F32, kind="ExternalInput").ap() for k, a in arrays.items()}
    y = nc.dram_tensor("y", [B, C, T], F32, kind="ExternalOutput").ap()
    scratch = nc.dram_tensor("w_pairs", [PAIRS + 1, P, 2 * CT * 3 * P], F16).ap()
    scratch_b = nc.dram_tensor("b_pairs", [PAIRS + 1, P, 2], F32).ap()
    build(nc, ap["x"], {k[2:]: v for k, v in ap.items() if k.startswith("w_")}, y, ap["consts"], scratch, scratch_b)
    r = run_bass_kernel_spmd(nc, [arrays], core_ids=[0])
    return np.asarray(r.results[0]["y"]).reshape(B, C, 32, 32)
```

```python
from contextlib import ExitStack

import numpy as np
import concourse.bass as bass
from concourse import mybir

F32 = mybir.dt.float32
F16 = mybir.dt.float16
ALU = mybir.AluOpType
ACT = mybir.ActivationFunctionType
AX = mybir.AxisListType
ABSMAX = bass.bass_isa.ReduceOp.max

P = 128
B, C, T = 8, 512, 1024
CT = C // P
TT = T // P
HALF = 512
HEADS = 8
CH = C // HEADS
PAIRS = HEADS // 2
GROUP = C // 32
EPS0, EPS1 = 1e-5, 1e-6

WSC = 512.0
ZSC = 64.0
QSC = 1.0 / (WSC * ZSC * 2)
PSC = 4096.0

UNITS_PAIR = 2 * TT
UNITS0 = PAIRS * UNITS_PAIR
UNITS = UNITS0 + TT
QUARTERS = TT // 2
PV_PAIR = QUARTERS
PV0 = PAIRS * PV_PAIR
PVS = PV0 + 2 * QUARTERS
FILL = 6
G_PROJ0 = (PAIRS - 1) * FILL
G_PROJ1 = G_PROJ0 + CT
G_G = G_PROJ1 + CT
G_U = G_G + 2 * CT
G_NEXT = G_U + TT
GROUPS = G_NEXT + FILL
SPLITS = GROUPS - 2 * CT
STACK_INC = 4 * 16
V_INC = W_QK_INC = 2 * 16
W_V_INC = 16

LAG0 = 3
HI_LAG = 2
PV_LAG = UNITS_PAIR // QUARTERS + LAG0 + 1
STEPS0 = UNITS_PAIR + PV_LAG + 1
AHEAD = 8
SLOTS = 4


def spread_chunks(first_step, per_step):
    steps, n = {}, 0
    for st, k in enumerate(per_step, first_step):
        steps[st] = [divmod(n + i, 4) for i in range(k)]
        n += k
    return steps


FILL_CHUNKS = spread_chunks(1, (1, 1, 1, 1, 1, 1, 2, 2, 2, 1, 1, 1, 1, 2, 2, 2, 2))
PROJ_CHUNKS = spread_chunks(17, (2,) * 8)
NEXT_CHUNKS = spread_chunks(4, (4,) * FILL)
NEXT_AHEAD = {9: (0, 1), 10: (2,), 11: (3, 4, 5, 6, 7)}
STEPS1 = TT + 4
NORM_PARTS = {m: (2 * (m - TT + CT), 2 * (m - TT + CT) + 1) for m in range(TT - CT, TT)}


def finished(chunks, st):
    return [j for j, i in chunks.get(st, ()) if i == 3]


def group_count(b, m):
    return b * GROUPS + (FILL + m + 1)


def split_count(b, m):
    return b * SPLITS + (FILL + (m if m < G_PROJ0 else m - 2 * CT) + 1)


def unit_count(b, n):
    return b * UNITS + (n + 1)


def used_pv(b, v):
    return b * PVS + (v + 3)


def pair_unit(u):
    return (u % 4) // 2, 2 * (u // 4) + u % 2


def build(nc, x, w, y, consts, scratch, scratch_b):
    ctx = ExitStack()
    with ctx:
        def sb(name, cols, dt=F32):
            return ctx.enter_context(nc.sbuf_tensor(name, [P, cols], dt))

        def sem(name):
            return ctx.enter_context(nc.semaphore(name))

        def f16(ap):
            return ap.bitcast(F16)

        xin = sb("xin", CT * T)
        r2 = sb("x1_att", 2 * CT * T)
        r1 = sb("probs_t", 8192)
        r3 = sb("stacks_probs", 8192)
        z0buf = sb("z0", CT * T)
        natbuf = sb("nat", 3072)
        globuf = sb("g_lo", 2048)
        stgbuf = sb("staging", 2 * HALF)
        pvsbuf = sb("pv_staging", 2 * HALF)
        zstbuf = sb("z_staging", 2 * T)
        wcurbuf = sb("wqkv_pair", 1538)
        wp0 = sb("wp0", 2 * CT * C, F16)
        wm1 = sb("wm1", 2 * CT * C, F16)
        wu1 = sb("wu1", 2 * CT * C, F16)
        cst = sb("ident_gavg", 2 * P)
        ident16 = sb("ident16", P, F16)
        vec = sb("vectors", 64)
        small = sb("small", 160)

        xin_v = xin[:, :].rearrange("p (c t) -> p c t", c=CT)
        x1 = r2[:, 0:CT * T].rearrange("p (c t) -> p c t", c=CT)
        att = f16(r2[:, CT * T:]).rearrange("p (s c t) -> p s c t", s=2, c=CT)
        z1 = att
        z0 = f16(z0buf[:, :]).rearrange("p (s c t) -> p s c t", s=2, c=CT)
        probs_t = f16(r1[:, :]).rearrange("p (k h s j t) -> p k h s j t", k=2, h=2, s=2, j=TT)
        u_t = [f16(r1[:, 4096 * s + 2048:4096 * s + 4096]).rearrange("p (j o) -> p j o", j=TT) for s in range(2)]
        stacks = f16(r3[:, 0:3072]).rearrange("p (s h t) -> p s h t", s=3, h=2)
        v_cur = f16(r3[:, 3072:4096]).rearrange("p (s j c) -> p s j c", s=2, j=TT)
        probs32 = [r3[:, 4096:5120], r3[:, 5120:6144], zstbuf[:, 0:T], zstbuf[:, T:2 * T]]
        probs_hi = [f16(r3[:, 6144:6656]), f16(r3[:, 6656:7168]), f16(globuf[:, 0:512]), f16(globuf[:, 512:1024])]
        probs_lo = [f16(r3[:, 7168:7680]), f16(r3[:, 7680:8192]), f16(globuf[:, 1024:1536]), f16(globuf[:, 1536:2048])]
        g_s = [f16(r3[:, 0:2048]).rearrange("p (c t) -> p c t", c=CT),
               f16(globuf[:, :]).rearrange("p (c t) -> p c t", c=CT)]
        qk_nat = f16(natbuf[:, 0:2048]).rearrange("p (n s t) -> p n s t", n=2, s=2)
        v_nat = f16(natbuf[:, 2048:3072]).rearrange("p (s j c) -> p s j c", s=2, j=TT)
        stg = stgbuf[:, :].rearrange("p (k t) -> p k t", k=2)
        pvs = pvsbuf[:, :].rearrange("p (k t) -> p k t", k=2)
        zst = zstbuf[:, :].rearrange("p (k t) -> p k t", k=CT)
        w_qk = f16(wcurbuf[:, 0:1024]).rearrange("p (s c n o) -> p s c n o", s=2, c=CT, n=2)
        w_v = f16(wcurbuf[:, 1024:1536]).rearrange("p (s c o) -> p s c o", s=2, c=CT)
        b_cur = wcurbuf[:, 1536:1538]
        wp0_v = wp0[:, :].rearrange("p (s c o) -> p s c o", s=2, c=CT)
        wm1_v = wm1[:, :].rearrange("p (s c o) -> p s c o", s=2, c=CT)
        wu1_v = wu1[:, :].rearrange("p (s c o) -> p s c o", s=2, c=CT)
        ident = cst[:, 0:P]
        gavg = cst[:, P:2 * P]

        w0t = r2[:, 0:6144].rearrange("p (c o) -> p c o", c=CT)
        wp0t = r2[:, 6144:8192].rearrange("p (c o) -> p c o", c=CT)
        wq1, wk1, wv1 = (r3[:, 2048 * i:2048 * i + 2048].rearrange("p (j c) -> p j c", j=CT) for i in range(3))
        m_raw = z0buf[:, 0:2048].rearrange("p (c o) -> p c o", c=CT)
        u_raw = z0buf[:, 2048:4096].rearrange("p (c o) -> p c o", c=CT)
        wp1t = globuf[:, :].rearrange("p (c o) -> p c o", c=CT)
        gain_row = stgbuf[:, 0:C]
        w0s = [f16(r1[:, 3072 * s:3072 * s + 3072]).rearrange("p (c n j o) -> p c n j o", c=CT, n=3, j=PAIRS)
               for s in range(2)]

        wp0_scaled = r1[:, 6144:8192].rearrange("p (c o) -> p c o", c=CT)
        m_gained, u_gained = (wide[:, :].bitcast(F32).rearrange("p (c o) -> p c o", c=CT) for wide in (wm1, wu1))

        gain0, shift0 = vec[:, 0:4], vec[:, 4:8]
        bqkv, bp0_in = vec[:, 8:20], vec[:, 20:24]
        gain1, shift1 = vec[:, 24:28], vec[:, 28:32]
        bq1, bv1, bp1_in = vec[:, 32:36], vec[:, 36:40], vec[:, 40:44]
        b_qkv = small[:, 0:12]
        b_g = small[:, 12:16]
        b_out1 = small[:, 16:20]
        b_out0 = small[:, 20:24]
        tops = small[:, 24:28]
        inv = small[:, 28:32]
        exp_scale = small[:, 32:34]
        out_scale = small[:, 34:36]
        b_qk = small[:, 36:44].rearrange("p (n j) -> p n j", n=2)
        tmp = small[:, 52:76]
        neg_half = small[:, 76:80]
        neg_max = small[:, 80:82]
        exp_bias = small[:, 82:84]
        row_sum = small[:, 84:86]
        row_inv = small[:, 86:88]
        row_scaled = small[:, 88:90]
        gn_stats = sb("gn_stats", CT * 12)
        gn = small[:, 96:144].rearrange("p (k c) -> p k c", c=CT)
        gn_sub = sb("gn_sub", 4 * CT)
        gn_parts = gn_stats[:, :].rearrange("p (c s k) -> p c s k", c=CT, s=4)

        scores = ctx.enter_context(nc.psum_tensor("scores", [P, 2, 2, HALF], F32))
        trans = ctx.enter_context(nc.psum_tensor("transposed", [P, 2, T], F16))
        pv = ctx.enter_context(nc.psum_tensor("pv", [P, HALF], F32))
        proj = ctx.enter_context(nc.psum_tensor("proj", [P, HALF], F32))
        group_sums = scores[:, 0, 0, 0:2 * CT]

        loaded_qk, loaded_vp, loadedv = sem("loaded_qk"), sem("loaded_vp"), sem("loadedv")
        loaded_w0, loaded_wp0 = sem("loaded_w0"), sem("loaded_wp0")
        bank_filled, bank_read = sem("bank_filled"), sem("bank_read")
        bias_sums0, bias_sums1, bias0_ready, bias_proj = (sem("bias_sums0"), sem("bias_sums1"), sem("bias0_ready"),
                                                          sem("bias_proj"))
        factor0_ready, factor1_ready = sem("factor0_ready"), sem("factor1_ready")
        w_scaled, hi_for_pool, lo_by_pool = sem("w_scaled"), sem("hi_for_pool"), sem("lo_by_pool")
        tops_in, tops_out = sem("tops_in"), sem("tops_out")
        setup_chain = sem("setup_chain")
        w0_split, w0_stored = sem("w0_split"), sem("w0_stored")
        x_loaded = sem("x_loaded")
        pvs_full, pvs_used = sem("pvs_full"), sem("pvs_used")

        with nc.Block() as block:
            @block.sync
            def _(sp):
                def load_weights(dst, name, done):
                    sp.dma_start(dst, w[name].rearrange("(j p) c -> p j c", p=P)).then_inc(done, 16)

                load_weights(wq1, "q1", loaded_qk)
                load_weights(wk1, "k1", loaded_qk)
                sp.dma_start(vec[:, 0:44], w["vectors"]).then_inc(loadedv, 16)
                sp.dma_start(cst[:, :], consts).then_inc(loadedv, 16)
                sp.dma_start(gain_row, w["gain1"].rearrange("(a n) -> a n", a=1).broadcast_to([P, C]))\
                  .then_inc(loadedv, 16)
                load_weights(w0t, "qkv_t", loaded_w0)
                load_weights(wv1, "v1", loaded_vp)
                load_weights(wp1t, "p1_t", loaded_vp)
                load_weights(wp0t, "p0_t", loaded_wp0)
                sp.dma_start(xin_v, x[0].rearrange("(c p) t -> p c t", p=P)).then_inc(x_loaded, 16)
                sp.wait_ge(w0_split, CT)
                for s in range(2):
                    for p in range(PAIRS + 1):
                        half = scratch[p, :, s * 1536:s * 1536 + 1536]
                        sp.dma_start(half.rearrange("p (c n o) -> p c n o", c=CT, n=3),
                                     w0s[s][:, :, :, p % PAIRS, :]).then_inc(w0_stored, 16)
                for p in range(PAIRS + 1):
                    sp.dma_start(scratch_b[p], b_qk[:, :, p % PAIRS], allow_slow_non_contiguous=True)\
                      .then_inc(w0_stored, 16)
                sp.wait_ge(w0_stored, 3 * (PAIRS + 1) * 16)

            @block.gpsimd
            def _(pool):
                nc.gpsimd.memset(neg_half, -0.5).then_inc(pvs_used, 2)
                pool.wait_ge(tops_in, 1)
                nc.gpsimd.partition_all_reduce(tops[:, 0:2], tmp[:, 0:2], P, ABSMAX).then_inc(tops_out, 1)
                pool.wait_ge(hi_for_pool, 1)
                nc.gpsimd.tensor_tensor(wp0_v[:, 1], wp0_scaled, wp0_v[:, 0], ALU.subtract).then_inc(lo_by_pool, 1)
                pool.wait_ge(tops_in, 2)
                nc.gpsimd.partition_all_reduce(tops[:, 2:4], tmp[:, 2:4], P, ABSMAX).then_inc(tops_out, 1)
                pool.wait_ge(hi_for_pool, 2)
                nc.gpsimd.tensor_tensor(wu1_v[:, 1], u_raw, wu1_v[:, 0], ALU.subtract).then_inc(lo_by_pool, 1)

            @block.tensor
            def _(pe):
                banks = [scores[:, k // 2, k % 2, :] for k in range(4)]
                def product(a_nat, b_v, fills):
                    for c, fill in enumerate(fills):
                        if fill >= CT:
                            pe.wait_ge(bank_read, fill - CT + 1)
                        for k in range(CT):
                            last = nc.tensor.matmul(banks[fill % CT], a_nat[:, k, c * P:c * P + P], b_v[:, k, :],
                                                    start=(k == 0), stop=(k == CT - 1))
                        last.then_inc(bank_filled, 1)

                def vector_sums(col, pairs):
                    for o in range(CT):
                        for k, (a, v) in enumerate(pairs):
                            for c in range(CT):
                                last = nc.tensor.matmul(proj[:, col + o:col + o + 1], a[:, c, o * P:o * P + P],
                                                        v[:, c:c + 1], start=(k + c == 0),
                                                        stop=(k == len(pairs) - 1 and c == CT - 1))
                    return last

                pe.wait_ge(loaded_qk, 2 * 16)
                product(wq1, wk1, range(CT))
                pe.wait_ge(loadedv, 3 * 16)
                pe.wait_ge(loaded_w0, 16)
                for n in range(3):
                    last = vector_sums(CT * n, [(w0t[:, :, n * C:n * C + C], shift0)])
                last.then_inc(bias_sums0, 1)
                pe.wait_ge(loaded_vp, 2 * 16)
                product(wv1, wp1t, range(CT, 2 * CT))
                pe.wait_ge(bank_read, 2 * CT)
                vector_sums(12, [(m_raw, shift1), (wk1, bq1)])
                vector_sums(16, [(u_raw, shift1), (wp1t, bv1)]).then_inc(bias_sums1, 1)
                pe.wait_ge(loaded_wp0, 16)
                pe.wait_ge(bias0_ready, 1)
                for o in range(CT):
                    for c in range(CT):
                        last = nc.tensor.matmul(pv[:, o:o + 1], wp0t[:, c, o * P:o * P + P], b_qkv[:, 8 + c:9 + c],
                                                start=(c == 0), stop=(c == CT - 1))
                last.then_inc(bias_proj, 1)

            @block.scalar
            def _(act):
                banks = [scores[:, k // 2, k % 2, :] for k in range(4)]
                def keep_product(raw, fills):
                    for c, fill in enumerate(fills):
                        act.wait_ge(bank_filled, fill + 1)
                        nc.scalar.activation(raw[:, c, :], banks[fill % CT], ACT.Copy).then_inc(bank_read, 1)

                keep_product(m_raw, range(CT))
                act.wait_ge(loadedv, 3 * 16)
                nc.scalar.activation(ident16[:, :], ident, ACT.Copy).then_inc(pvs_full, 1)
                act.wait_ge(factor0_ready, 1)
                for c in range(CT):
                    nc.scalar.activation(w0t[:, c, :], w0t[:, c, :], ACT.Copy, scale=tmp[:, 12 + c:13 + c])\
                      .then_inc(w_scaled, 1)
                keep_product(u_raw, range(CT, 2 * CT))
                nc.scalar.activation(wp0_scaled, wp0t, ACT.Copy, scale=inv[:, 1:2]).then_inc(w_scaled, 1)
                act.wait_ge(factor1_ready, 1)
                nc.scalar.activation(u_raw, u_gained, ACT.Copy, scale=inv[:, 3:4]).then_inc(w_scaled, 1)
                nc.scalar.activation(m_raw, m_gained, ACT.Copy, scale=inv[:, 2:3]).then_inc(w_scaled, 1)

            @block.vector
            def _(dve):
                chain = 0

                def step(ins):
                    nonlocal chain
                    chain += 1
                    ins.then_inc(setup_chain, 1)
                    dve.wait_ge(setup_chain, chain)

                v = nc.vector
                def top(dst, src, axes):
                    step(v.tensor_reduce(dst, src, axes, ALU.max, apply_absolute_value=True))

                dve.wait_ge(loadedv, 3 * 16)
                dve.wait_ge(loaded_w0, 16)
                for c in range(CT):
                    top(tmp[:, 8 + c:9 + c], w0t[:, c, :], AX.X)
                step(v.tensor_tensor(tmp[:, 8:12], tmp[:, 8:12], gain0, ALU.mult))
                top(tmp[:, 0:1], tmp[:, 8:12], AX.X)
                dve.wait_ge(loaded_wp0, 16)
                top(tmp[:, 1:2], wp0t, AX.XY)
                dve.wait_ge(bias_sums0, 1)
                v.tensor_tensor(b_qkv, proj[:, 0:12], bqkv, ALU.add).then_inc(bias0_ready, 1)
                dve.wait_ge(bias0_ready, 1)
                top(tmp[:, 4:5], b_qkv, AX.X)
                v.tensor_tensor(tmp[:, 0:1], tmp[:, 0:1], tmp[:, 4:5], ALU.max).then_inc(tops_in, 1)
                dve.wait_ge(tops_out, 1)
                step(v.tensor_scalar(tops[:, 0:2], tops[:, 0:2], 1e-30, None, ALU.max))
                step(v.reciprocal(tmp[:, 4:6], tops[:, 0:2]))
                step(v.tensor_scalar(inv[:, 0:2], tmp[:, 4:6], WSC, None, ALU.mult))
                v.tensor_scalar(tmp[:, 12:16], gain0, inv[:, 0:1], None, ALU.mult).then_inc(factor0_ready, 1)
                step(v.tensor_scalar(tmp[:, 16:17], tmp[:, 4:5], 0.5, None, ALU.mult))
                step(v.tensor_scalar(small[:, 36:44], b_qkv[:, 0:8], tmp[:, 16:17], None, ALU.mult))
                step(v.tensor_tensor(tmp[:, 6:8], tops[:, 0:2], tops[:, 0:1].broadcast_to([P, 2]), ALU.mult))
                step(v.tensor_scalar(exp_scale[:, 0:1], tmp[:, 6:7], 4.0 / CH ** 0.5, None, ALU.mult))
                step(v.tensor_scalar(out_scale[:, 0:1], tmp[:, 7:8], 2.0 / WSC, None, ALU.mult))
                for c in range(CT):
                    hi, lo = (w0s[k][:, c].rearrange("p n j o -> p (n j o)") for k in range(2))
                    dve.wait_ge(w_scaled, c + 1)
                    step(v.tensor_copy(hi, w0t[:, c, :]))
                    v.tensor_tensor(lo, w0t[:, c, :], hi, ALU.subtract).then_inc(w0_split, 1)
                for c in range(CT):
                    dve.wait_ge(bank_read, c + 1)
                    step(v.scalar_tensor_tensor(m_gained[:, c, :], m_raw[:, c, :], gain1[:, c:c + 1], gain_row,
                                                ALU.mult, ALU.mult))
                top(tmp[:, 2:3], m_gained, AX.XY)
                for c in range(CT):
                    dve.wait_ge(bank_read, CT + c + 1)
                    step(v.tensor_scalar(u_gained[:, c, :], u_raw[:, c, :], gain1[:, c:c + 1], None, ALU.mult))
                top(tmp[:, 3:4], u_gained, AX.XY)
                dve.wait_ge(w_scaled, CT + 1)
                v.tensor_copy(wp0_v[:, 0], wp0_scaled).then_inc(hi_for_pool, 1)
                dve.wait_ge(bias_sums1, 1)
                step(v.tensor_tensor(b_g, proj[:, 12:16], gain1, ALU.mult))
                step(v.tensor_tensor(b_out1, proj[:, 16:20], bp1_in, ALU.add))
                top(tmp[:, 5:6], b_g, AX.X)
                v.tensor_tensor(tmp[:, 2:3], tmp[:, 2:3], tmp[:, 5:6], ALU.max).then_inc(tops_in, 1)
                dve.wait_ge(tops_out, 2)
                step(v.tensor_scalar(tops[:, 2:4], tops[:, 2:4], 1e-30, None, ALU.max))
                step(v.reciprocal(tmp[:, 4:6], tops[:, 2:4]))
                v.tensor_scalar(inv[:, 2:4], tmp[:, 4:6], WSC, None, ALU.mult).then_inc(factor1_ready, 1)
                step(v.tensor_scalar(tmp[:, 17:18], tmp[:, 4:5], 0.5, None, ALU.mult))
                step(v.tensor_scalar(b_g, b_g, tmp[:, 17:18], None, ALU.mult))
                step(v.tensor_scalar(exp_scale[:, 1:2], tops[:, 2:3], 2.0 / (ZSC * C ** 0.5), None, ALU.mult))
                step(v.tensor_scalar(out_scale[:, 1:2], tops[:, 3:4], 2.0 / PSC, None, ALU.mult))
                dve.wait_ge(w_scaled, CT + 2)
                v.tensor_copy(wu1_v[:, 0], u_raw).then_inc(hi_for_pool, 1)
                dve.wait_ge(w_scaled, CT + 3)
                step(v.tensor_copy(wm1_v[:, 0], m_raw))
                step(v.tensor_tensor(wm1_v[:, 1], m_raw, wm1_v[:, 0], ALU.subtract))
                dve.wait_ge(bias_proj, 1)
                v.tensor_tensor(b_out0, pv[:, 0:4], bp0_in, ALU.add)

        y_stored = sem("y_stored")
        w_qk_loaded, w_v_loaded = sem("w_qk_loaded"), sem("w_v_loaded")
        stack_a, stack_b, v_moved = sem("stack_a"), sem("stack_b"), sem("v_moved")
        scores_done, neg_max_done, bias_done = sem("scores_done"), sem("neg_max_done"), sem("bias_done")
        exp_done, sum_scaled, inv_done = sem("exp_done"), sem("sum_scaled"), sem("inv_done")
        rescaled, rescaled_dve = sem("rescaled"), sem("rescaled_dve")
        hi_done, lo_done = sem("hi_done"), sem("lo_done")
        trans_hi, trans_lo = sem("trans_hi"), sem("trans_lo")
        kept_hi, kept_lo = sem("kept_hi"), sem("kept_lo")
        pv_done, pvs_hi = sem("pv_done"), sem("pvs_hi")
        group_done, stg_full, stg_hi, stg_used = sem("group_done"), sem("stg_full"), sem("stg_hi"), sem("stg_used")
        gn_in, gn_out, gn_chain = sem("gn_in"), sem("gn_out"), sem("gn_chain")
        pow_in, pow_out, z_coef = sem("pow_in"), sem("pow_out"), sem("z_coef")
        z32_done, z_hi, z_done0, z_done1 = sem("z32_done"), sem("z_hi"), sem("z_done0"), sem("z_done1")
        GN_CHAIN = 7

        def per_batch(eng, body):
            with eng.Fori(0, B - 1) as b:
                body(b, False)
            body(B - 1, True)

        def per_pair(eng, b, body):
            with eng.Fori(0, PAIRS - 2) as p:
                body(p, False, False)
            body(PAIRS - 2, False, True)
            body(PAIRS - 1, True, False)

        def probs_t_of(u, s):
            head, tile = pair_unit(u)
            return probs_t[:, (u // 4) % 2, head, s, :, (tile % 2) * P:(tile % 2) * P + P]

        def by_act(u):
            return u % 4 != 3

        def free_within(v0):
            def free(u):
                return v0 + u // 4 - 1 if u % 4 == 0 and u >= 8 else None
            return free

        def free_across(v0):
            return lambda u: v0 - 1 if u == 0 else v0 if u == 4 else None

        def free_next_batch(v0):
            return lambda u: v0 if u == 2 else v0 - 2 if u == 0 else None

        def free1(v0, u):
            return v0 + 2 * (u // 2 - 1) if u % 2 == 0 and u >= 4 else None

        def free_nothing(u):
            return None

        def back(u):
            return SLOTS

        def back_first(u):
            return SLOTS if u >= SLOTS else None

        def back_next_batch(u):
            return 2 if u < 2 else SLOTS

        with nc.Block() as block:
            @block.sync
            def _(sp):
                def stacks_of(head, done):
                    rows = slice(head * CH, head * CH + CH)
                    low, high = slice(0, CH), slice(CH, P)
                    for dst, src in ((stacks[low, 1:3, head], qk_nat[rows, 1, :, :]),
                                     (stacks[high, 1:3, head], qk_nat[rows, 1, :, :]),
                                     (stacks[low, 0, head], qk_nat[rows, 0, 0, :]),
                                     (stacks[high, 0, head], qk_nat[rows, 0, 1, :])):
                        sp.dma_start(dst, src).then_inc(done, 16)

                def move_v(*halves):
                    for s in halves:
                        sp.dma_start(v_cur[:, s], v_nat[:, s]).then_inc(v_moved, 16)

                def load_x(b):
                    sp.dma_start(xin_v, x[b].rearrange("(c p) t -> p c t", p=P)).then_inc(x_loaded, 16)

                def w_pairs_of(p):
                    return scratch[p].rearrange("p (g m) -> p g m", m=3 * P)

                def load_w_qk(p):
                    sp.dma_start(w_qk.rearrange("p s c n o -> p (s c) (n o)"), w_pairs_of(p)[:, :, 0:2 * P])\
                     .then_inc(w_qk_loaded, 16)
                    sp.dma_start(b_cur, scratch_b[p]).then_inc(w_qk_loaded, 16)

                def load_w_v(p):
                    sp.dma_start(w_v.rearrange("p s c o -> p (s c) o"), w_pairs_of(p)[:, :, 2 * P:3 * P])\
                     .then_inc(w_v_loaded, 16)

                load_w_qk(0)
                load_w_v(0)
                sp.wait_ge(stg_used, 4)
                load_w_qk(1)
                stacks_of(0, stack_a)
                stacks_of(1, stack_b)
                sp.wait_ge(stg_used, FILL)
                move_v(0, 1)
                load_w_v(1)

                def batch(b, last):
                    def pair(p, last_pair, next_last):
                        bp = b * UNITS + p * UNITS_PAIR
                        if not last_pair:
                            sp.wait_ge(stg_used, b * GROUPS + p * FILL + (FILL + 4))
                            load_w_qk(p + 2)
                            sp.wait_ge(scores_done, bp + UNITS_PAIR - 2)
                            stacks_of(0, stack_a)
                            sp.wait_ge(scores_done, bp + UNITS_PAIR)
                            stacks_of(1, stack_b)
                            sp.wait_ge(group_done, b * GROUPS + p * FILL + 2 * FILL)
                            load_w_v(p + 2)
                            sp.wait_ge(stg_used, b * GROUPS + p * FILL + 2 * FILL)
                            sp.wait_ge(pv_done, b * PVS + p * PV_PAIR + PV_PAIR)
                            move_v(0, 1)

                    per_pair(sp, b, pair)
                    if not last:
                        sp.wait_ge(stg_used, group_count(b, G_G - 1))
                        load_x(b + 1)
                    for q in range(QUARTERS):
                        if q == 2 and not last:
                            sp.wait_ge(stg_used, group_count(b, G_NEXT + 3))
                            load_w_qk(1)
                            sp.wait_ge(scores_done, unit_count(b, UNITS - 1))
                            stacks_of(0, stack_a)
                            stacks_of(1, stack_b)
                        sp.wait_ge(pvs_used, used_pv(b, PV0 + 2 * q + 1))
                        cols = slice(256 * q, 256 * q + 256)
                        sp.dma_start(y[b].rearrange("(c p) t -> p c t", p=P)[:, :, cols], x1[:, :, cols])\
                          .then_inc(y_stored, 16)
                    if not last:
                        sp.wait_ge(stg_used, group_count(b, G_NEXT + 5))
                        load_w_v(1)
                        move_v(0)
                    sp.wait_ge(y_stored, (b * QUARTERS + QUARTERS) * 16)
                    if not last:
                        move_v(1)

                per_batch(sp, batch)

            @block.tensor
            def _(pe):
                THREE = ((0, 0), (0, 1), (1, 0))

                def products(out, terms, first, last):
                    for i, (lhs, rhs) in enumerate(terms):
                        for k, (a, c) in enumerate(THREE):
                            mm = nc.tensor.matmul(out, lhs(a), rhs(c), start=(first and i + k == 0),
                                                  stop=(last and i == len(terms) - 1 and k == 2))
                    return mm

                def group(out, terms):
                    return products(out, terms, True, True)

                def qkv_chunk(j, i):
                    if j < 4:
                        n, cols = (1, 0)[j // 2], slice((j % 2) * HALF, (j % 2) * HALF + HALF)
                        return products(proj[:, :], [(lambda s: w_qk[:, s, i, n, :], lambda s: z0[:, s, i, cols])],
                                        i == 0, i == 3)
                    rows = slice((4 * (j - 4) + i) * P, (4 * (j - 4) + i) * P + P)
                    return group(proj[:, i * P:i * P + P],
                                 [(lambda s, c=c: z0[:, s, c, rows], lambda s, c=c: w_v[:, s, c, :])
                                  for c in range(CT)])

                def qkv_chunks(chunks, count, loads):
                    for j, i in chunks:
                        if i == 0:
                            pe.wait_ge(stg_full, count + j)
                            if j == 0:
                                pe.wait_ge(w_qk_loaded, loads * W_QK_INC)
                            if j == 4:
                                pe.wait_ge(w_v_loaded, loads * W_V_INC)
                        mm = qkv_chunk(j, i)
                        if i == 3:
                            mm.then_inc(group_done, 1)

                def transpose(n, slot, s, first=False):
                    ready, done, kept = ((hi_done, trans_hi, kept_hi), (lo_done, trans_lo, kept_lo))[s]
                    src = (probs_hi, probs_lo)[s]
                    if not first:
                        pe.wait_ge(kept, n - 1)
                    pe.wait_ge(ready, n)
                    for j in range(TT):
                        last = nc.tensor.transpose(trans[:, s, j * P:j * P + P], src[slot][:, j * P:j * P + P],
                                                   ident16[:, :])
                    last.then_inc(done, 1)

                def scores0(n0, st, moved, prologue=False):
                    head, tile = pair_unit(st)
                    if st in (0, 2):
                        pe.wait_ge((stack_a, stack_b)[head], moved * STACK_INC)
                    if not (prologue and st < 2):
                        pe.wait_ge(exp_done, n0 + st - 1)
                    for half in range(2):
                        cols = slice(half * HALF, half * HALF + HALF)
                        for k in range(2):
                            mm = nc.tensor.matmul(scores[:, st % 2, half, :],
                                                  stacks[:, 0, head, tile * P:tile * P + P],
                                                  stacks[:, 1 + k, head, cols], start=(k == 0), stop=(k == 1))
                    mm.then_inc(scores_done, 1)

                def unit_step(n0, st, moved, prologue=False, between=lambda: None):
                    if st < UNITS_PAIR:
                        scores0(n0, st, moved, prologue)
                    u = st - LAG0
                    if 0 <= u < UNITS_PAIR:
                        transpose(n0 + (u + 1), u % SLOTS, 0, first=prologue and u == 0)
                    between()
                    if 0 <= u < UNITS_PAIR:
                        transpose(n0 + (u + 1), u % SLOTS, 1, first=prologue and u == 0)

                def gn_sum(n, k):
                    pe.wait_ge(gn_in, 2 * n + (k + 1))
                    nc.tensor.matmul(group_sums[:, k * CT:k * CT + CT], gavg, gn[:, 0, :] if k == 0 else gn[:, 3, :],
                                     start=True, stop=True).then_inc(gn_out, 1)

                gn_sum(0, 0)
                gn_sum(0, 1)
                pe.wait_ge(z_done0, CT)
                pe.wait_ge(w_qk_loaded, W_QK_INC)
                pe.wait_ge(w_v_loaded, W_V_INC)
                for j in range(FILL):
                    if j:
                        pe.wait_ge(stg_full, j)
                    if j == 1:
                        pe.wait_ge(z_done1, CT)
                    for i in range(4):
                        mm = qkv_chunk(j, i)
                    mm.then_inc(group_done, 1)
                for st in range(AHEAD):
                    unit_step(0, st, 1, prologue=True, between=lambda: qkv_chunks(FILL_CHUNKS.get(st, ()), FILL, 2))

                def batch(b, last):
                    def pair(p, last_pair, next_last):
                        n0 = b * UNITS + p * UNITS_PAIR
                        v0 = b * PVS + p * PV_PAIR
                        m0 = b * GROUPS + p * FILL + FILL
                        moved = b * PAIRS + p + 1

                        def pv_chunk(st):
                            for q in range(QUARTERS):
                                j = st - (4 * q + PV_LAG)
                                if 0 <= j < 4:
                                    if j == 0:
                                        pe.wait_ge(kept_hi, n0 + 4 * q + 4)
                                        pe.wait_ge(kept_lo, n0 + 4 * q + 4)
                                        pe.wait_ge(pvs_full, v0 + q + 1)
                                        if q == 0:
                                            pe.wait_ge(v_moved, moved * V_INC)
                                    for kt in (2 * j, 2 * j + 1):
                                        for i, (a, c) in enumerate(THREE):
                                            for head in range(2):
                                                mm = nc.tensor.matmul(
                                                    pv[head * CH:head * CH + CH, 0:256],
                                                    v_cur[:, a, kt, head * CH:head * CH + CH],
                                                    probs_t[:, q % 2, head, c, kt, :],
                                                    start=(kt == 0 and i == 0), stop=(kt == TT - 1 and i == 2))
                                    if j == 3:
                                        mm.then_inc(pv_done, 1)

                        def fill(st):
                            pv_chunk(st)
                            if not last_pair:
                                qkv_chunks(FILL_CHUNKS.get(st, ()), m0, b * PAIRS + p + 2)
                                if not next_last:
                                    qkv_chunks(FILL_CHUNKS.get(st - (STEPS0 - AHEAD), ()), m0 + FILL,
                                               b * PAIRS + p + 3)
                                return
                            for o, i in PROJ_CHUNKS.get(st, ()):
                                if o + i == 0:
                                    pe.wait_ge(pvs_used, used_pv(b, p * PV_PAIR + 1))
                                if i == 0:
                                    pe.wait_ge(stg_full, group_count(b, G_PROJ0 + o - 1))
                                mm = out_proj_chunk(o, 0, proj, i)
                                if i == 3:
                                    mm.then_inc(group_done, 1)

                        for st in range(AHEAD, STEPS0):
                            ahead = st - (STEPS0 - AHEAD)
                            if last_pair or ahead < 0:
                                unit_step(n0, st, moved, between=lambda: fill(st))
                            else:
                                unit_step(n0, st, moved)
                                unit_step(n0 + UNITS_PAIR, ahead, moved + 1, between=lambda: fill(st))

                    def out_proj_chunk(o, half, bank, i):
                        cols = slice(half * HALF, half * HALF + HALF)
                        return products(bank[:, :], [(lambda s: wp0_v[:, s, i, o * P:o * P + P],
                                                      lambda s: att[:, s, i, cols])], i == 0, i == 3)

                    per_pair(pe, b, pair)

                    banks = (proj, pv)
                    for o in range(CT):
                        pe.wait_ge(stg_full, group_count(b, G_PROJ1 + o - (1 if o == 0 else 2)))
                        for i in range(4):
                            if o == 0 and i == PAIRS - 1:
                                pe.wait_ge(pvs_used, used_pv(b, PV0 - 1))
                            mm = out_proj_chunk(o, 1, banks[o % 2], i)
                        mm.then_inc(group_done, 1)
                    gn_sum(b * 2 + 1, 0)
                    gn_sum(b * 2 + 1, 1)
                    def g_chunk(m, c):
                        half, o = m // CT, m % CT
                        cols = slice(half * HALF, half * HALF + HALF)
                        mm = products(banks[m % 2][:, :], [(lambda s: wm1_v[:, s, c, o * P:o * P + P],
                                                            lambda s: z1[:, s, c, cols])], c == 0, c == CT - 1)
                        if c == CT - 1:
                            mm.then_inc(group_done, 1)

                    pe.wait_ge(stg_full, group_count(b, G_G - 1))
                    for c in range(CT):
                        pe.wait_ge(z_done0, (b * 2 + 1) * CT + (c + 1))
                        g_chunk(0, c)
                        g_chunk(1, c)
                    for m in range(2, 2 * CT):
                        pe.wait_ge(stg_full, group_count(b, G_G + m - 2))
                        for c in range(CT):
                            if m == CT:
                                pe.wait_ge(z_done1, (b * 2 + 1) * CT + (c + 1))
                            g_chunk(m, c)
                    for m in range(TT):
                        if not last and m in (1, 2):
                            gn_sum(b * 2 + 2, m - 1)
                        pe.wait_ge(stg_full, group_count(b, G_U + m - 2))
                        group(banks[m % 2][:, :], [(lambda s, c=c: z1[:, s, c, m * P:m * P + P],
                                                    lambda s, c=c: wu1_v[:, s, c, :]) for c in range(CT)])\
                            .then_inc(group_done, 1)

                    n0 = b * UNITS + UNITS0
                    v0 = b * PVS + PV0
                    for st in range(STEPS1):
                        if st < TT:
                            if st == 0:
                                pe.wait_ge(stg_used, group_count(b, G_U - 1))
                                if not last:
                                    pe.wait_ge(pow_in, b * 2 + 3)
                            pe.wait_ge(exp_done, n0 + st - 1)
                            for half in range(2):
                                cols = slice(half * HALF, half * HALF + HALF)
                                mm = group(scores[:, st % 2, half, :],
                                           [(lambda s, c=c: g_s[s][:, c, st * P:st * P + P],
                                             lambda s, c=c: z1[:, s, c, cols]) for c in range(CT)])
                            mm.then_inc(scores_done, 1)
                        if not last and st in NEXT_CHUNKS:
                            if st == 4:
                                pe.wait_ge(z_done0, (b * 2 + 3) * CT)
                                pe.wait_ge(z_done1, (b * 2 + 3) * CT)
                            qkv_chunks(NEXT_CHUNKS[st], group_count(b, G_NEXT - 1), b * PAIRS + (PAIRS + 1))
                        if not last and st in NEXT_AHEAD and st < 11:
                            for nst in NEXT_AHEAD[st]:
                                unit_step(b * UNITS + UNITS, nst, b * PAIRS + (PAIRS + 1),
                                          between=lambda: qkv_chunks(FILL_CHUNKS.get(nst, ()), group_count(b, GROUPS - 1),
                                                                     b * PAIRS + (PAIRS + 2)))
                        for q in range(QUARTERS):
                            for k in range(2):
                                if st == 2 * q + 3 + k:
                                    if k == 0:
                                        pe.wait_ge(kept_hi, n0 + 2 * q + 2)
                                        pe.wait_ge(kept_lo, n0 + 2 * q + 2)
                                    if q == 0 and k == 0:
                                        pe.wait_ge(stg_used, group_count(b, G_NEXT - 1))
                                    pe.wait_ge(pvs_full, v0 + 2 * q + k + 1)
                                    for i in range(2):
                                        o = 2 * k + i
                                        mm = group(pv[:, 256 * i:256 * i + 256],
                                                   [(lambda s, kt=kt: u_t[s][:, kt, o * P:o * P + P],
                                                     lambda s, kt=kt: probs_t[:, q % 2, 0, s, kt, :])
                                                    for kt in range(TT)])
                                    mm.then_inc(pv_done, 1)
                        if not last and st == 11:
                            for nst in NEXT_AHEAD[st]:
                                unit_step(b * UNITS + UNITS, nst, b * PAIRS + (PAIRS + 1),
                                          between=lambda: qkv_chunks(FILL_CHUNKS.get(nst, ()), group_count(b, GROUPS - 1),
                                                                     b * PAIRS + (PAIRS + 2)))
                        u = st - 1
                        if 0 <= u < TT:
                            transpose(n0 + (u + 1), u % 2, 0)
                            transpose(n0 + (u + 1), u % 2, 1)

                per_batch(pe, batch)

            @block.scalar
            def _(act):
                def exponentials(n, par, slot, layer, back):
                    act.wait_ge(bias_done, n)
                    if back is not None:
                        act.wait_ge(lo_done, n - back)
                    nc.scalar.activation(probs32[slot], scores[:, par, :, :].rearrange("p a t -> p (a t)"), ACT.Exp,
                                         bias=exp_bias[:, par:par + 1], scale=exp_scale[:, layer:layer + 1],
                                         accum_out=row_sum[:, par:par + 1]).then_inc(exp_done, 1)

                def rescale(n, par, slot):
                    act.wait_ge(inv_done, n)
                    nc.scalar.activation(probs32[slot], probs32[slot], ACT.Copy, scale=row_inv[:, par:par + 1])\
                      .then_inc(rescaled, 1)

                def keep_lo(n, dst, free):
                    act.wait_ge(trans_lo, n)
                    if free is not None:
                        act.wait_ge(pv_done, free)
                    nc.scalar.activation(dst, trans[:, 1, :].rearrange("p (j t) -> p j t", j=TT), ACT.Copy)\
                      .then_inc(kept_lo, 1)

                def unit_step(n0, st, free, back, between=lambda: None):
                    if st < UNITS_PAIR:
                        exponentials(n0 + (st + 1), st % 2, st % SLOTS, 0, back(st))
                    between()
                    u = st - 1
                    if 0 <= u < UNITS_PAIR and by_act(u):
                        rescale(n0 + (u + 1), u % 2, u % SLOTS)
                    u = st - LAG0
                    if 0 <= u < UNITS_PAIR:
                        keep_lo(n0 + (u + 1), probs_t_of(u, 1), free(u))

                def stage(count, m, src, scale, bias, two_back=True):
                    act.wait_ge(group_done, count)
                    if two_back:
                        act.wait_ge(stg_used, count - 2)
                    if bias is None:
                        nc.scalar.activation(stg[:, m % 2, :], src, ACT.Copy, scale=scale).then_inc(stg_full, 1)
                    else:
                        nc.scalar.activation(stg[:, m % 2, :], src, ACT.Identity, scale=scale, bias=bias)\
                          .then_inc(stg_full, 1)

                def qkv_stage(count, j, two_back=True):
                    n = (1, 0)[j // 2] if j < 4 else None
                    bias = None if n is None else b_cur[:, n:n + 1]
                    stage(count, j, proj[:, :], QSC, bias, two_back)

                def fill_stages(st, count):
                    for j in finished(FILL_CHUNKS, st):
                        qkv_stage(count + (j + 1), j)

                def normalise(src, count, parts=range(2 * CT), first=False):
                    for n in parts:
                        half, c = n // CT, n % CT
                        if n == 0:
                            act.wait_ge(z_coef, count)
                        if half == 1:
                            act.wait_ge(z_done0, (count - 1) * CT + (c + 1))
                        elif not first:
                            act.wait_ge(z_done1, (count - 2) * CT + (c + 1))
                        nc.scalar.activation(zst[:, c, :], src[:, c, half * HALF:half * HALF + HALF], ACT.Identity,
                                             scale=gn[:, 8, c:c + 1], bias=gn[:, 9, c:c + 1]).then_inc(z32_done, 1)

                act.wait_ge(x_loaded, 16)
                normalise(xin_v, 1, first=True)
                for j in range(FILL):
                    qkv_stage(j + 1, j, two_back=j >= 2)
                for st in range(AHEAD):
                    unit_step(0, st, free_nothing, back_first, between=lambda: fill_stages(st, FILL))

                def batch(b, last):
                    def pair(p, last_pair, next_last):
                        n0 = b * UNITS + p * UNITS_PAIR
                        v0 = b * PVS + p * PV_PAIR
                        m0 = b * GROUPS + p * FILL + FILL
                        def others(st):
                            for q in range(QUARTERS):
                                if st == 4 * q + PV_LAG + 3:
                                    act.wait_ge(pv_done, v0 + (q + 1))
                                    act.wait_ge(pvs_used, v0 + (q + 1))
                                    nc.scalar.activation(pvs[:, q % 2, 0:256], pv[:, 0:256], ACT.Copy, scale=1.0 / PSC)\
                                      .then_inc(pvs_full, 1)
                            if not last_pair:
                                fill_stages(st, m0)
                                if not next_last:
                                    fill_stages(st - (STEPS0 - AHEAD), m0 + FILL)
                            else:
                                for o in finished(PROJ_CHUNKS, st):
                                    stage(group_count(b, G_PROJ0 + o), o, proj[:, :], out_scale[:, 0:1],
                                          b_out0[:, o:o + 1])

                        for st in range(AHEAD, STEPS0):
                            ahead = st - (STEPS0 - AHEAD)
                            if last_pair or ahead < 0:
                                unit_step(n0, st, free_within(v0), back, between=lambda: others(st))
                            else:
                                unit_step(n0, st, free_within(v0), back)
                                unit_step(n0 + UNITS_PAIR, ahead, free_across(v0 + PV_PAIR), back,
                                          between=lambda: others(st))

                    per_pair(act, b, pair)
                    banks = (proj, pv)
                    for o in range(CT):
                        stage(group_count(b, G_PROJ1 + o), o, banks[o % 2][:, :], out_scale[:, 0:1], b_out0[:, o:o + 1])
                    normalise(x1, b * 2 + 2)
                    for m in range(2 * CT):
                        stage(group_count(b, G_G + m), m, banks[m % 2][:, :], QSC, b_g[:, m % CT:m % CT + 1])
                    for m in range(TT):
                        stage(group_count(b, G_U + m), m, banks[m % 2][:, :], QSC, None)
                        if not last and m >= TT - CT:
                            normalise(xin_v, b * 2 + 3, NORM_PARTS[m])
                    n0 = b * UNITS + UNITS0
                    v0 = b * PVS + PV0
                    for st in range(STEPS1):
                        if 0 <= st - 1 < TT and by_act(st - 1):
                            rescale(n0 + st, (st - 1) % 2, (st - 1) % 2)
                        if st < TT:
                            exponentials(n0 + (st + 1), st % 2, st % 2, 1, 2)
                        if not last:
                            for j in finished(NEXT_CHUNKS, st):
                                qkv_stage(group_count(b, G_NEXT + j), j)
                            if st in NEXT_AHEAD and st < 11:
                                for nst in NEXT_AHEAD[st]:
                                    unit_step(b * UNITS + UNITS, nst, free_next_batch(b * PVS + PVS), back_next_batch,
                                              between=lambda: fill_stages(nst, group_count(b, GROUPS - 1)))
                        for q in range(QUARTERS):
                            for k in range(2):
                                if st == 2 * q + 3 + k:
                                    act.wait_ge(pv_done, v0 + (2 * q + k + 1))
                                    act.wait_ge(pvs_used, v0 + (2 * q + k + 1))
                                    for i in range(2):
                                        o = 2 * k + i
                                        cp = nc.scalar.activation(pvs[:, k, 256 * i:256 * i + 256],
                                                                  pv[:, 256 * i:256 * i + 256], ACT.Identity,
                                                                  scale=out_scale[:, 1:2], bias=b_out1[:, o:o + 1])
                                    cp.then_inc(pvs_full, 1)
                        if not last and st == 11:
                            for nst in NEXT_AHEAD[st]:
                                unit_step(b * UNITS + UNITS, nst, free_next_batch(b * PVS + PVS), back_next_batch,
                                              between=lambda: fill_stages(nst, group_count(b, GROUPS - 1)))
                        u = st - 1
                        if 0 <= u < TT:
                            keep_lo(n0 + (u + 1), probs_t[:, (u // 2) % 2, 0, 1, :, (u % 2) * P:(u % 2) * P + P],
                                    free1(v0, u))

                per_batch(act, batch)

            @block.vector
            def _(dve):
                v = nc.vector

                def row_max(n, par):
                    dve.wait_ge(scores_done, n)
                    v.tensor_reduce(neg_max[:, par:par + 1], scores[:, par, :, :], AX.XY, ALU.max, negate=True)\
                     .then_inc(neg_max_done, 1)

                def row_bias(n, par, layer):
                    dve.wait_ge(neg_max_done, n)
                    v.tensor_scalar(exp_bias[:, par:par + 1], neg_max[:, par:par + 1], exp_scale[:, layer:layer + 1],
                                    None, ALU.mult).then_inc(bias_done, 1)

                def scale_sum(n, par):
                    dve.wait_ge(exp_done, n)
                    v.tensor_scalar(row_scaled[:, par:par + 1], row_sum[:, par:par + 1], 1.0 / PSC, None, ALU.mult)\
                     .then_inc(sum_scaled, 1)

                def invert_sum(n, par):
                    dve.wait_ge(sum_scaled, n)
                    v.reciprocal(row_inv[:, par:par + 1], row_scaled[:, par:par + 1]).then_inc(inv_done, 1)

                def split(n, f0, u, slot, back):
                    if by_act(u):
                        dve.wait_ge(rescaled, 3 * f0 + (3 * (u // 4) + u % 4 + 1))
                    else:
                        dve.wait_ge(inv_done, n)
                        v.tensor_scalar(probs32[slot], probs32[slot], row_inv[:, u % 2:u % 2 + 1], None, ALU.mult)\
                         .then_inc(rescaled_dve, 1)
                        dve.wait_ge(rescaled_dve, f0 + (u // 4 + 1))
                    if back is not None:
                        dve.wait_ge(trans_hi, n - back)
                    v.tensor_copy(probs_hi[slot], probs32[slot]).then_inc(hi_done, 1)

                def keep_hi(n, dst, free):
                    dve.wait_ge(trans_hi, n)
                    if free is not None:
                        dve.wait_ge(pv_done, free)
                    v.tensor_copy(dst, trans[:, 0, :].rearrange("p (j t) -> p j t", j=TT)).then_inc(kept_hi, 1)

                def unit_step(n0, f0, st, free, back):
                    if 0 <= st - 1 < UNITS_PAIR:
                        scale_sum(n0 + st, (st - 1) % 2)
                    if st < UNITS_PAIR:
                        row_max(n0 + (st + 1), st % 2)
                    if 0 <= st - 1 < UNITS_PAIR:
                        invert_sum(n0 + st, (st - 1) % 2)
                    if st < UNITS_PAIR:
                        row_bias(n0 + (st + 1), st % 2, 0)
                    u = st - HI_LAG
                    if 0 <= u < UNITS_PAIR:
                        split(n0 + (u + 1), f0, u, u % SLOTS, back(u))
                    u = st - LAG0
                    if 0 <= u < UNITS_PAIR:
                        keep_hi(n0 + (u + 1), probs_t_of(u, 0), free(u))

                def group_hi(dst, m, count):
                    dve.wait_ge(stg_full, count)
                    v.tensor_copy(dst, stg[:, m % 2, :]).then_inc(stg_hi, 1)

                def qkv_hi(j, count):
                    if j < 4:
                        cols = slice((j % 2) * HALF, (j % 2) * HALF + HALF)
                        group_hi(qk_nat[:, (1, 0)[j // 2], 0, cols], j, count)
                    else:
                        group_hi(v_nat[:, 0, 4 * (j - 4):4 * (j - 4) + 4, :].rearrange("p j c -> p (j c)"), j, count)

                def fill_his(st, count):
                    for j in finished(FILL_CHUNKS, st):
                        qkv_hi(j, count + (j + 1))

                def stats(src, c, half):
                    v.bn_stats(gn_stats[:, c * 12 + half * 6:c * 12 + half * 6 + 6],
                               src[:, c, half * HALF:half * HALF + HALF]).then_inc(gn_chain, 1)

                part_mean, part_sq = gn_parts[:, :, :, 1], gn_parts[:, :, :, 2]
                mean_dist = gn_sub[:, :].rearrange("p (c s) -> p c s", c=CT)
                g_mean, spread, g_var, rough, t = (gn[:, i, :] for i in (2, 3, 4, 5, 6))

                def gn_step(k, i, ins):
                    ins.then_inc(gn_chain, 1)
                    dve.wait_ge(gn_chain, k * (8 + GN_CHAIN) + (8 + i))

                def norm_means(k):
                    dve.wait_ge(gn_chain, k * (8 + GN_CHAIN) + 8)
                    v.tensor_reduce(gn[:, 0, :], part_mean, AX.X, ALU.add).then_inc(gn_in, 1)

                def norm_variances(k):
                    dve.wait_ge(gn_out, 2 * k + 1)
                    gn_step(k, 1, v.tensor_scalar(g_mean, group_sums[:, 0:CT], 0.25, None, ALU.mult))
                    gn_step(k, 2, v.tensor_tensor(mean_dist, part_mean, g_mean.rearrange("p (c s) -> p c s", s=1)
                                                  .broadcast_to([P, CT, 4]), ALU.subtract))
                    gn_step(k, 3, v.tensor_tensor(mean_dist, mean_dist, mean_dist, ALU.mult))
                    gn_step(k, 4, v.scalar_tensor_tensor(mean_dist, mean_dist, T / 4.0, part_sq, ALU.mult, ALU.add))
                    v.tensor_reduce(spread, mean_dist, AX.X, ALU.add).then_inc(gn_in, 1)

                def norm_scales(k, eps):
                    dve.wait_ge(gn_out, 2 * k + 2)
                    v.tensor_scalar(g_var, group_sums[:, CT:2 * CT], 1.0 / T, eps, ALU.mult, ALU.add).then_inc(pow_in, 1)
                    dve.wait_ge(pow_out, k + 1)
                    gn_step(k, 5, v.tensor_tensor(t, rough, rough, ALU.mult))
                    gn_step(k, 6, v.scalar_tensor_tensor(t, t, -0.5 * ZSC, g_var, ALU.mult, ALU.mult))
                    gn_step(k, 7, v.scalar_tensor_tensor(gn[:, 8, :], t, 1.5 * ZSC, rough, ALU.add, ALU.mult))
                    v.scalar_tensor_tensor(gn[:, 9, :], g_mean, -1.0, gn[:, 8, :], ALU.mult, ALU.mult)\
                     .then_inc(z_coef, 1)

                def norm_split(dst, k, parts=range(2 * CT)):
                    for m in parts:
                        half, c = m // CT, m % CT
                        cols = slice(half * HALF, half * HALF + HALF)
                        n = k * 2 * CT + (m + 1)
                        dve.wait_ge(z32_done, n)
                        v.tensor_copy(dst[:, 0, c, cols], zst[:, c, :]).then_inc(z_hi, 1)
                        if half == 0:
                            dve.wait_ge(z_hi, n)
                            v.tensor_tensor(dst[:, 1, c, cols], zst[:, c, :], dst[:, 0, c, cols], ALU.subtract)\
                             .then_inc(z_done0, 1)

                def all_stats(src):
                    for c in range(CT):
                        for half in range(2):
                            stats(src, c, half)

                dve.wait_ge(x_loaded, 16)
                all_stats(xin_v)
                norm_means(0)
                norm_variances(0)
                norm_scales(0, EPS0)
                norm_split(z0, 0)
                for j in range(FILL):
                    qkv_hi(j, j + 1)
                for st in range(AHEAD):
                    unit_step(0, 0, st, free_nothing, back_first)
                    fill_his(st, FILL)

                def batch(b, last):
                    def pair(p, last_pair, next_last):
                        n0 = b * UNITS + p * UNITS_PAIR
                        v0 = b * PVS + p * PV_PAIR
                        m0 = b * GROUPS + p * FILL + FILL
                        f0 = b * (UNITS // 4) + p * (UNITS_PAIR // 4)
                        for st in range(AHEAD, STEPS0):
                            unit_step(n0, f0, st, free_within(v0), back)
                            ahead = st - (STEPS0 - AHEAD)
                            if not last_pair and ahead >= 0:
                                unit_step(n0 + UNITS_PAIR, f0 + UNITS_PAIR // 4, ahead, free_across(v0 + PV_PAIR), back)
                            if not last_pair:
                                fill_his(st, m0)
                                if not next_last:
                                    fill_his(st - (STEPS0 - AHEAD), m0 + FILL)
                            for q in range(QUARTERS):
                                if st == 4 * q + PV_LAG + 4:
                                    dve.wait_ge(pvs_full, v0 + (q + 2))
                                    v.tensor_copy(att[:, 0, bass.ds(p, 1), 256 * q:256 * q + 256].rearrange("p a t -> p (a t)")
                                                  if not isinstance(p, int) else att[:, 0, p, 256 * q:256 * q + 256],
                                                  pvs[:, q % 2, 0:256]).then_inc(pvs_hi, 1)

                    per_pair(dve, b, pair)
                    for c in range(CT):
                        dve.wait_ge(stg_used, group_count(b, G_PROJ0 + c))
                        stats(x1, c, 0)
                    for c in range(CT):
                        count = group_count(b, G_PROJ1 + c)
                        dve.wait_ge(stg_full, count)
                        v.tensor_tensor(x1[:, c, HALF:T], stg[:, c % 2, :], xin_v[:, c, HALF:T], ALU.add)\
                         .then_inc(stg_used, 1)
                        dve.wait_ge(stg_used, count)
                        stats(x1, c, 1)
                    norm_means(b * 2 + 1)
                    norm_variances(b * 2 + 1)
                    norm_scales(b * 2 + 1, EPS1)
                    norm_split(z1, b * 2 + 1)
                    for m in range(2 * CT):
                        half, o = m // CT, m % CT
                        group_hi(g_s[0][:, o, half * HALF:half * HALF + HALF], m, group_count(b, G_G + m))
                        if not last and m >= CT:
                            if m == CT:
                                dve.wait_ge(x_loaded, (b + 2) * 16)
                            stats(xin_v, m - CT, 0)
                            stats(xin_v, m - CT, 1)
                    if not last:
                        norm_means(b * 2 + 2)
                    for m in range(TT):
                        group_hi(u_t[0][:, m, :], m, group_count(b, G_U + m))
                        if not last and m == 0:
                            norm_variances(b * 2 + 2)
                        if not last and m == 1:
                            norm_scales(b * 2 + 2, EPS0)
                        if not last and m >= TT - CT:
                            norm_split(z0, b * 2 + 2, NORM_PARTS[m])
                    n0 = b * UNITS + UNITS0
                    f0 = b * (UNITS // 4) + UNITS0 // 4
                    v0 = b * PVS + PV0
                    for st in range(STEPS1):
                        u = st - 1
                        if 0 <= u < TT:
                            scale_sum(n0 + (u + 1), u % 2)
                            invert_sum(n0 + (u + 1), u % 2)
                            split(n0 + (u + 1), f0, u, u % 2, 2)
                        if st < TT:
                            row_max(n0 + (st + 1), st % 2)
                            row_bias(n0 + (st + 1), st % 2, 1)
                        if not last:
                            for j in finished(NEXT_CHUNKS, st):
                                qkv_hi(j, group_count(b, G_NEXT + j))
                            if st in NEXT_AHEAD:
                                for nst in NEXT_AHEAD[st]:
                                    unit_step(b * UNITS + UNITS, b * (UNITS // 4) + UNITS // 4, nst,
                                              free_next_batch(b * PVS + PVS), back_next_batch)
                                    fill_his(nst, group_count(b, GROUPS - 1))
                        if 0 <= u < TT:
                            keep_hi(n0 + (u + 1), probs_t[:, (u // 2) % 2, 0, 0, :, (u % 2) * P:(u % 2) * P + P],
                                    free1(v0, u))

                per_batch(dve, batch)

            @block.gpsimd
            def _(pool):
                g = nc.gpsimd

                def group_lo(lo, hi, m, count):
                    pool.wait_ge(stg_hi, count)
                    g.tensor_tensor(lo, stg[:, m % 2, :], hi, ALU.subtract).then_inc(stg_used, 1)

                def qkv_lo(j, count):
                    if j < 4:
                        n, cols = (1, 0)[j // 2], slice((j % 2) * HALF, (j % 2) * HALF + HALF)
                        group_lo(qk_nat[:, n, 1, cols], qk_nat[:, n, 0, cols], j, count)
                    else:
                        rows = slice(4 * (j - 4), 4 * (j - 4) + 4)
                        group_lo(v_nat[:, 1, rows, :].rearrange("p j c -> p (j c)"),
                                 v_nat[:, 0, rows, :].rearrange("p j c -> p (j c)"), j, count)

                def fill_los(st, count):
                    for j in finished(FILL_CHUNKS, st):
                        qkv_lo(j, count + (j + 1))

                def residual0(b, m, c, half):
                    pool.wait_ge(stg_full, group_count(b, m))
                    cols = slice(half * HALF, half * HALF + HALF)
                    g.tensor_tensor(x1[:, c, cols], stg[:, m % 2, :], xin_v[:, c, cols], ALU.add).then_inc(stg_used, 1)

                def rough_rsqrt(k):
                    pool.wait_ge(pow_in, k + 1)
                    g.tensor_tensor(gn[:, 5, :], gn[:, 4, :], neg_half, ALU.pow).then_inc(pow_out, 1)

                def split_lo(n, slot, back):
                    pool.wait_ge(hi_done, n)
                    if back is not None:
                        pool.wait_ge(trans_lo, n - back)
                    g.tensor_tensor(probs_lo[slot], probs32[slot], probs_hi[slot], ALU.subtract).then_inc(lo_done, 1)

                def unit_step(n0, st, back):
                    u = st - HI_LAG
                    if 0 <= u < UNITS_PAIR:
                        split_lo(n0 + (u + 1), u % SLOTS, back(u))

                def norm_lo(dst, k, tiles=range(CT)):
                    for c in tiles:
                        pool.wait_ge(z_hi, k * 2 * CT + (CT + c + 1))
                        g.tensor_tensor(dst[:, 1, c, HALF:T], zst[:, c, :], dst[:, 0, c, HALF:T], ALU.subtract)\
                         .then_inc(z_done1, 1)

                rough_rsqrt(0)
                norm_lo(z0, 0)
                for j in range(FILL):
                    qkv_lo(j, j + 1)
                for st in range(AHEAD):
                    unit_step(0, st, back_first)
                    fill_los(st, FILL)

                def batch(b, last):
                    def pair(p, last_pair, next_last):
                        v0 = b * PVS + p * PV_PAIR
                        s0 = b * SPLITS + p * FILL + FILL
                        n0 = b * UNITS + p * UNITS_PAIR
                        for st in range(AHEAD, STEPS0):
                            unit_step(n0, st, back)
                            ahead = st - (STEPS0 - AHEAD)
                            if not last_pair and ahead >= 0:
                                unit_step(n0 + UNITS_PAIR, ahead, back)
                            if not last_pair:
                                fill_los(st, s0)
                                if not next_last:
                                    fill_los(st - (STEPS0 - AHEAD), s0 + FILL)
                            else:
                                for o in finished(PROJ_CHUNKS, st):
                                    residual0(b, G_PROJ0 + o, o, 0)
                            for q in range(QUARTERS):
                                if st == 4 * q + PV_LAG + 4:
                                    cols = slice(256 * q, 256 * q + 256)
                                    at = [att[:, s, bass.ds(p, 1), cols].rearrange("p a t -> p (a t)")
                                          if not isinstance(p, int) else att[:, s, p, cols] for s in range(2)]
                                    pool.wait_ge(pvs_hi, b * PV0 + p * PV_PAIR + (q + 1))
                                    g.tensor_tensor(at[1], pvs[:, q % 2, 0:256], at[0], ALU.subtract)\
                                     .then_inc(pvs_used, 1)

                    per_pair(pool, b, pair)
                    rough_rsqrt(b * 2 + 1)
                    norm_lo(z1, b * 2 + 1)
                    for m in range(2 * CT):
                        half, o = m // CT, m % CT
                        cols = slice(half * HALF, half * HALF + HALF)
                        group_lo(g_s[1][:, o, cols], g_s[0][:, o, cols], m, split_count(b, G_G + m))
                    for m in range(TT):
                        group_lo(u_t[1][:, m, :], u_t[0][:, m, :], m, split_count(b, G_U + m))
                        if not last and m == 1:
                            rough_rsqrt(b * 2 + 2)
                        if not last and m >= TT - CT:
                            norm_lo(z0, b * 2 + 2, [n - CT for n in NORM_PARTS[m] if n >= CT])
                    for st in range(STEPS1):
                        if 0 <= st - 1 < TT:
                            split_lo(b * UNITS + (UNITS0 + st), (st - 1) % 2, 2)
                        if not last:
                            for j in finished(NEXT_CHUNKS, st):
                                qkv_lo(j, split_count(b, G_NEXT + j))
                            for nst in NEXT_AHEAD.get(st, ()):
                                unit_step(b * UNITS + UNITS, nst, back_next_batch)
                                fill_los(nst, split_count(b, GROUPS - 1))
                        for q in range(QUARTERS):
                            for k in range(2):
                                if st == 2 * q + 3 + k:
                                    pool.wait_ge(pvs_full, b * PVS + (PV0 + 2 * q + k + 2))
                                    xs = x1[:, 2 * k:2 * k + 2, 256 * q:256 * q + 256]
                                    g.tensor_tensor(xs, pvs[:, k, :].rearrange("p (i t) -> p i t", i=2), xs, ALU.add)\
                                     .then_inc(pvs_used, 1)

                per_batch(pool, batch)


_VECTORS = ("L0_conv_norm_w", "L0_conv_norm_b", "L0_conv_qkv_b", "L0_conv_proj_b", "L1_conv_gn_gamma",
            "L1_conv_gn_beta", "L1_conv_q_b", "L1_conv_v_b", "L1_conv_proj_b")


def kernel(**inputs):
    import concourse.bacc as bacc
    from concourse.bass_utils import run_bass_kernel_spmd

    nc = bacc.Bacc("TRN2", target_bir_lowering=False, num_devices=1)
    norm_group = np.arange(P) // GROUP
    same = norm_group[:, None] == norm_group[None, :]


    def by_kind(a):
        a = np.asarray(a)
        return a.reshape(HEADS, 3, CH, -1).swapaxes(0, 1).reshape(a.shape)

    vectors = {n: np.asarray(inputs[n]) for n in _VECTORS}
    vectors["L0_conv_qkv_b"] = by_kind(inputs["L0_conv_qkv_b"])
    arrays = {
        "x": np.asarray(inputs["x"]).reshape(B, C, T),
        "consts": np.concatenate([np.eye(P), same / GROUP], axis=1).astype(np.float32),
        "w_vectors": np.concatenate([vectors[n].reshape(-1, P).T for n in _VECTORS], axis=1),
        "w_gain1": np.asarray(inputs["L1_conv_gn_gamma"]),
        "w_qkv_t": by_kind(inputs["L0_conv_qkv_w"]).T,
        "w_p0_t": np.asarray(inputs["L0_conv_proj_w"]).T,
        "w_q1": np.asarray(inputs["L1_conv_q_w"]),
        "w_k1": np.asarray(inputs["L1_conv_k_w"]),
        "w_v1": np.asarray(inputs["L1_conv_v_w"]),
        "w_p1_t": np.asarray(inputs["L1_conv_proj_w"]).T,
    }
    arrays = {k: np.ascontiguousarray(a) for k, a in arrays.items()}
    ap = {k: nc.dram_tensor(k, list(a.shape), F32, kind="ExternalInput").ap() for k, a in arrays.items()}
    y = nc.dram_tensor("y", [B, C, T], F32, kind="ExternalOutput").ap()
    scratch = nc.dram_tensor("w_pairs", [PAIRS + 1, P, 2 * CT * 3 * P], F16).ap()
    scratch_b = nc.dram_tensor("b_pairs", [PAIRS + 1, P, 2], F32).ap()
    build(nc, ap["x"], {k[2:]: v for k, v in ap.items() if k.startswith("w_")}, y, ap["consts"], scratch, scratch_b)
    r = run_bass_kernel_spmd(nc, [arrays], core_ids=[0])
    return np.asarray(r.results[0]["y"]).reshape(B, C, 32, 32)
```
